# Optimizing a Trainium2 kernel written in Bass

```python
import numpy as np
import jax
import jax.numpy as jnp

def _softmax(x, axis=-1):
    return jax.nn.softmax(x, axis=axis)

def _gelu(x):
    return jax.nn.gelu(x, approximate=True)

def _silu(x):
    return jax.nn.silu(x)

def _sigmoid(x):
    return jax.nn.sigmoid(x)

def _layernorm(x, axis=-1, eps=1e-05):
    m = jnp.mean(x, axis=axis, keepdims=True)
    v = jnp.var(x, axis=axis, keepdims=True)
    return (x - m) / jnp.sqrt(v + eps)

def _scatter_add(tgt, idx, src, axis=0):
    return tgt.at[idx].add(src)

def _segment_sum(src, seg, n):
    return jax.ops.segment_sum(src, seg, n)
kernel_name = 'mk_xattn_ffn_d1_seqx_r4_db638b'

def setup_inputs(seed: int=0):
    np.random.seed(seed)
    _w = jnp.asarray

    def _rec_inputs():
        import jax
        import jax.numpy as jnp
        _rk = jax.random.key(seed)
        x = -0.0002928 + 1 * jax.random.normal(jax.random.fold_in(_rk, 1), (16, 256, 256), jnp.float32)
        _lenS = 256 - jax.random.randint(jax.random.fold_in(_rk, 7), (16,), 0, max(1, 256 // 4) + 1, jnp.int32)
        _lenS2 = 256 - jax.random.randint(jax.random.fold_in(_rk, 8), (16,), 0, max(1, 256 // 4) + 1, jnp.int32)
        _ctx_1024P = jax.random.normal(jax.random.fold_in(_rk, 11), (16, 16, 256), jnp.float32)
        _ctx_1024c = jax.random.dirichlet(jax.random.fold_in(_rk, 511), 0.3 * jnp.ones((16,), jnp.float32), (16, 256))
        _ctx_1024t = jnp.einsum('bsk,bkd->bsd', _ctx_1024c, _ctx_1024P)
        _ctx_1024t = _ctx_1024t * jax.lax.rsqrt(jnp.mean(jnp.square(_ctx_1024t)) + 1e-12) * 0.953939
        ctx_1024 = -1.39393e-06 + 0.999914 * (_ctx_1024t + 0.3 * jax.random.normal(jax.random.fold_in(_rk, 611), (16, 256, 256), jnp.float32))
        return (x, ctx_1024)
    x, ctx_1024 = _rec_inputs()

    def _L0_xattn_setup():
        import jax, jax.numpy as jnp
        import numpy as np
        EPS = 1e-06
        LN_EPS = 1e-06

        def _mlstm_parallel_stabilized(q, k, v, igate_preact, fgate_preact):
            B, NH, S, DH = q.shape
            log_fg = jax.nn.log_sigmoid(fgate_preact[..., 0])
            cs = jnp.cumsum(log_fg, axis=-1)
            fg_mat = cs[..., :, None] - cs[..., None, :]
            mask = jnp.tril(jnp.ones((S, S), dtype=bool))
            log_D = jnp.where(mask, fg_mat + igate_preact[..., 0][..., None, :], -jnp.inf)
            max_log_D = jnp.max(log_D, axis=-1, keepdims=True)
            D = jnp.exp(log_D - max_log_D)
            k_scaled = k / jnp.sqrt(jnp.float32(DH)).astype(k.dtype)
            qk = jnp.einsum('bhsd,bhtd->bhst', q, k_scaled)
            C = qk * D
            normalizer = jnp.maximum(jnp.abs(jnp.sum(C, axis=-1, keepdims=True)), jnp.exp(-max_log_D))
            C_norm = C / (normalizer + EPS)
            return jnp.einsum('bhst,bhtd->bhsd', C_norm, v)

        def _multihead_layernorm(x, weight):
            mu = jnp.mean(x, axis=-1, keepdims=True)
            var = jnp.mean(jnp.square(x - mu), axis=-1, keepdims=True)
            xn = (x - mu) * jax.lax.rsqrt(var + LN_EPS)
            return xn * weight[None, :, None, :]
        key = jax.random.key(seed)
        ks = jax.random.split(key, 6)
        B, S, E, NH = (2, 512, 256, 8)
        q = jax.random.normal(ks[0], (B, S, E), dtype=jnp.float32)
        k = jax.random.normal(ks[1], (B, S, E), dtype=jnp.float32)
        v = jax.random.normal(ks[2], (B, S, E), dtype=jnp.float32)
        igate_kernel = jnp.zeros((3 * E, NH), dtype=jnp.float32)
        igate_bias = 0.1 * jax.random.normal(ks[3], (NH,), dtype=jnp.float32)
        fgate_kernel = jnp.zeros((3 * E, NH), dtype=jnp.float32)
        fgate_bias = jnp.linspace(3.0, 6.0, NH, dtype=jnp.float32)
        outnorm_weight = jnp.ones((NH, E // NH), dtype=jnp.float32)
        return {'q': q, 'k': k, 'v': v, 'igate_kernel': igate_kernel, 'igate_bias': igate_bias, 'fgate_kernel': fgate_kernel, 'fgate_bias': fgate_bias, 'outnorm_weight': outnorm_weight}
    _L0_xattn_all = _L0_xattn_setup()
    _L0_xattn_in = {k: v for k, v in _L0_xattn_all.items() if k in ('igate_kernel', 'igate_bias', 'fgate_kernel', 'fgate_bias', 'outnorm_weight')}
    del _L0_xattn_all

    def _L0_ffn_setup():
        import jax, jax.numpy as jnp
        import numpy as np
        TOP_K = 2
        key = jax.random.key(seed)
        k1, k2, k3, k4 = jax.random.split(key, 4)
        B, T, D, H, E = (2, 512, 256, 512, 8)
        x = jax.random.normal(k1, (B, T, D), dtype=jnp.float32)
        w12 = jax.random.normal(k2, (E, 2 * H, D), dtype=jnp.float32) * D ** (-0.5)
        w3 = jax.random.normal(k3, (E, D, H), dtype=jnp.float32) * H ** (-0.5)
        gate_w = jax.random.normal(k4, (E, D), dtype=jnp.float32) * D ** (-0.5)
        return {'x': x, 'w12': w12, 'w3': w3, 'gate_w': gate_w}
    _L0_ffn_all = _L0_ffn_setup()
    _L0_ffn_in = {k: v for k, v in _L0_ffn_all.items() if k in ('w12', 'w3', 'gate_w')}
    del _L0_ffn_all
    return {'x': x, 'ctx_1024': ctx_1024, 'L0_xattn_igate_kernel': _L0_xattn_in['igate_kernel'], 'L0_xattn_igate_bias': _L0_xattn_in['igate_bias'], 'L0_xattn_fgate_kernel': _L0_xattn_in['fgate_kernel'], 'L0_xattn_fgate_bias': _L0_xattn_in['fgate_bias'], 'L0_xattn_outnorm_weight': _L0_xattn_in['outnorm_weight'], 'L0_ffn_w12': _L0_ffn_in['w12'], 'L0_ffn_w3': _L0_ffn_in['w3'], 'L0_ffn_gate_w': _L0_ffn_in['gate_w']}

def reference(x, ctx_1024, L0_xattn_igate_kernel, L0_xattn_igate_bias, L0_xattn_fgate_kernel, L0_xattn_fgate_bias, L0_xattn_outnorm_weight, L0_ffn_w12, L0_ffn_w3, L0_ffn_gate_w):
    import jax
    import jax.numpy as jnp

    def _L0_xattn_ref(q, k, v, igate_kernel, igate_bias, fgate_kernel, fgate_bias, outnorm_weight):
        import jax, jax.numpy as jnp
        import numpy as np
        EPS = 1e-06
        LN_EPS = 1e-06

        def _mlstm_parallel_stabilized(q, k, v, igate_preact, fgate_preact):
            B, NH, S, DH = q.shape
            log_fg = jax.nn.log_sigmoid(fgate_preact[..., 0])
            cs = jnp.cumsum(log_fg, axis=-1)
            fg_mat = cs[..., :, None] - cs[..., None, :]
            mask = jnp.tril(jnp.ones((S, S), dtype=bool))
            log_D = jnp.where(mask, fg_mat + igate_preact[..., 0][..., None, :], -jnp.inf)
            max_log_D = jnp.max(log_D, axis=-1, keepdims=True)
            D = jnp.exp(log_D - max_log_D)
            k_scaled = k / jnp.sqrt(jnp.float32(DH)).astype(k.dtype)
            qk = jnp.einsum('bhsd,bhtd->bhst', q, k_scaled)
            C = qk * D
            normalizer = jnp.maximum(jnp.abs(jnp.sum(C, axis=-1, keepdims=True)), jnp.exp(-max_log_D))
            C_norm = C / (normalizer + EPS)
            return jnp.einsum('bhst,bhtd->bhsd', C_norm, v)

        def _multihead_layernorm(x, weight):
            mu = jnp.mean(x, axis=-1, keepdims=True)
            var = jnp.mean(jnp.square(x - mu), axis=-1, keepdims=True)
            xn = (x - mu) * jax.lax.rsqrt(var + LN_EPS)
            return xn * weight[None, :, None, :]
        B, S, E = q.shape
        NH = igate_bias.shape[0]
        qkv = jnp.concatenate([q, k, v], axis=-1)
        igate_preact = qkv @ igate_kernel + igate_bias
        fgate_preact = qkv @ fgate_kernel + fgate_bias
        qh = q.reshape(B, S, NH, -1).transpose(0, 2, 1, 3)
        kh = k.reshape(B, S, NH, -1).transpose(0, 2, 1, 3)
        vh = v.reshape(B, S, NH, -1).transpose(0, 2, 1, 3)
        ig = igate_preact.transpose(0, 2, 1)[..., None]
        fg = fgate_preact.transpose(0, 2, 1)[..., None]
        h = _mlstm_parallel_stabilized(qh, kh, vh, ig, fg)
        h_norm = _multihead_layernorm(h, outnorm_weight)
        return h_norm.transpose(0, 2, 1, 3).reshape(B, S, -1)

    def _L0_ffn_ref(x, w12, w3, gate_w):
        import jax, jax.numpy as jnp
        import numpy as np
        TOP_K = 2
        E = gate_w.shape[0]
        H = w3.shape[-1]
        scores = jnp.einsum('btd,ed->bte', x, gate_w)
        topk_scores, topk_idx = jax.lax.top_k(scores, TOP_K)
        topk_probs = jax.nn.softmax(topk_scores, axis=-1)
        total_probs = jnp.sum(jax.nn.one_hot(topk_idx, E, dtype=topk_probs.dtype) * topk_probs[..., None], axis=-2)
        h12 = jnp.einsum('btd,ehd->bteh', x, w12)
        h1, h2 = (h12[..., :H], h12[..., H:])
        hidden = jax.nn.silu(h1) * h2
        expert_out = jnp.einsum('bteh,edh->bted', hidden, w3)
        y = jnp.sum(total_probs[..., None] * expert_out, axis=-2)
        return y
    x = x + _L0_xattn_ref(_layernorm(x, axis=-1), ctx_1024, ctx_1024, L0_xattn_igate_kernel, L0_xattn_igate_bias, L0_xattn_fgate_kernel, L0_xattn_fgate_bias, L0_xattn_outnorm_weight)
    x = x + _L0_ffn_ref(_layernorm(x, axis=-1), L0_ffn_w12, L0_ffn_w3, L0_ffn_gate_w)
    return x

_drawn_inputs = setup_inputs


def setup_inputs(seed=0):
    import zlib

    import numpy as np

    out = dict(_drawn_inputs(seed))
    spreads = {'L0_xattn_igate_kernel': (0.0, 0.1),
     'L0_xattn_fgate_kernel': (0.0, 0.1),
     'L0_xattn_outnorm_weight': (1.0, 0.2)}
    factors = {'L0_xattn_igate_bias': 64.0}
    for name, (base, spread) in spreads.items():
        noise = np.random.default_rng([zlib.crc32(name.encode()), seed]).standard_normal(out[name].shape)
        drawn = base * np.exp(spread * noise) if base else spread * noise
        out[name] = jnp.asarray(drawn.astype(out[name].dtype))
    for name, factor in factors.items():
        out[name] = (out[name] * factor).astype(out[name].dtype)
    return out
```

```python
from contextlib import ExitStack

import numpy as np

import concourse.bass as bass
from concourse import mybir

ALU = mybir.AluOpType
ACT = mybir.ActivationFunctionType
AX = mybir.AxisListType
F32 = mybir.dt.float32
F32R = mybir.dt.float32r
BF16 = mybir.dt.bfloat16
I32 = mybir.dt.int32
U32 = mybir.dt.uint32

P = 128
B, S, E = 16, 256, 256
NH, DH = 8, 32
NE, HID = 8, 512
TOPK = 2
NC = S // P
NK = E // P
HG = P // DH
NG = NH // HG
DV = DH + 1
N = B * S
NT = N // P
TILES = (N * TOPK + NE * (P - 1)) // P
ROWS = N + P
ROW = E + NE
KH = HID // P
NX = 4
KS = float(DH) ** -0.5
LN_EPS, HEAD_EPS, NORM_EPS = 1e-5, 1e-6, 1e-6
PARTS = 3
MASKED = -1e30


def wait(eng, sem, value):
    if isinstance(value, int) and value <= 0:
        return
    eng.wait_ge(sem, value)


class Steps:

    def __init__(self, eng, sem, base):
        self.eng, self.sem, self.base, self.n = eng, sem, base, 0

    def then(self, ins):
        ins.then_inc(self.sem, 1)
        self.n += 1
        self.eng.wait_ge(self.sem, self.base + self.n)


def build(nc, x, ctx, ctxv, ctxT, gkq, gkk, gkv, ibias, fbias, onw, w12T, w3T, gateT, ident, identb,
          maskT, trib, marks, iota, out):
    qT_dram = nc.dram_tensor("qT_scratch", (B, P, NG, S), F32).ap()
    gate_dram = nc.dram_tensor("gate_scratch", (2 * NH, B, S), F32).ap()
    negM_dram = nc.dram_tensor("negM_scratch", (PARTS, B * NH, S), BF16).ap()
    g_dram = nc.dram_tensor("g_scratch", (PARTS, B * NH, S), BF16).ap()
    table = nc.dram_tensor("token_table", (ROWS, ROW), F32).ap()

    x_t = x.rearrange("(b c p) e -> b p c e", c=NC, p=P)
    ctx_t = ctx.rearrange("(b c p) e -> b p c e", c=NC, p=P)
    ctxv_t = ctxv.rearrange("(b c p) e -> b p c e", c=NC, p=P)
    ctxT_t = ctxT.rearrange("(k p) (b s) -> b p k s", p=P, s=S)
    out_t = out[0:N, :].rearrange("(b c p) e -> b p c e", c=NC, p=P)
    table_t = table[0:N, 0:E].rearrange("(b c p) e -> b p c e", c=NC, p=P)

    with ExitStack() as stack:
        def sb(name, shape, dt=F32, on=None):
            return (on or stack).enter_context(nc.sbuf_tensor(name, shape, dt))

        def sem(name):
            return stack.enter_context(nc.semaphore(name))

        bank = [stack.enter_context(nc.psum_tensor(f"bank{i}", [P, 512], F32)) for i in range(8)]

        w12h = sb("w12h", [P, NE, NK, 2 * HID], F32R)
        w12l = sb("w12l", [P, NE, NK, 2 * HID], F32R)
        id_f = sb("id_f", [P, P])
        id_b = sb("id_b", [P, P], BF16)
        tri = sb("tri", [P, 2, P], BF16)
        io = sb("io", [P, P + 2])
        gate_w = sb("gate_w", [P, NK, NE])
        scores = sb("scores", [P, NT, NE])
        etab = sb("etab", [P, TILES], I32)
        index = sb("index", [P, TILES], U32)

        early = ExitStack()
        cols = sb("cols", [P, 4, B * NH], on=early)
        neghalf = sb("neghalf", [P, NC * NH], on=early)
        onwb = sb("onwb", [P, NH, DH], on=early)
        mask4 = sb("mask4", [P, HG * P], BF16, on=early)
        wst = [sb(f"wst{i}", [P, HID], on=early) for i in range(4)]

        a = ExitStack()
        gq, gk, gv, gc = (sb(n, [P, NK, 2 * NH], on=a) for n in ("gq", "gk", "gv", "gc"))
        ib, fb = (sb(n, [P, 1], on=a) for n in ("ib", "fb"))
        X1 = [sb(f"x1_{i}", [P, NC, E], on=a) for i in range(2)]
        CT1 = [sb(f"ct1_{i}", [P, NK, S], on=a) for i in range(2)]
        Q1 = [sb(f"q1_{i}", [P, NC, E], on=a) for i in range(2)]
        QT1 = [sb(f"qt1_{i}", [P, NK, S], on=a) for i in range(2)]
        GS1 = [sb(f"gs1_{i}", [2 * NH, S], on=a) for i in range(2)]
        st1 = [sb(f"st1_{i}", [P, NC, 6], on=a) for i in range(2)]
        mv1 = [sb(f"mv1_{i}", [P, NC, 2], on=a) for i in range(2)]
        ve1 = [sb(f"ve1_{i}", [P, NC], on=a) for i in range(2)]
        rs1 = [sb(f"rs1_{i}", [P, NC], on=a) for i in range(2)]
        gi, gf, fa, fm, fe, fl, lsg, cs, g, M, negM, mx, zeros = (
            sb(n, [P, S], on=a) for n in ("gi", "gf", "fa", "fm", "fe", "fl", "lsg", "cs", "g_", "M_",
                                          "negM", "mx", "zeros"))
        dcol = sb("dcol", [P, 4, P], on=a)
        parts = sb("parts", [P, 2, PARTS, S], BF16, on=a)
        rest = sb("rest", [P, 2, PARTS - 1, S], on=a)
        zrow = sb("zrow", [P, ROW], on=a)
        a.close()

        m = ExitStack()
        X = [sb(f"x3_{i}", [P, NC, NH, DH], on=m) for i in range(2)]
        KT = [sb(f"kt{i}", [P, NG, S], on=m) for i in range(2)]
        QBD = [sb(f"qbd{i}", [P, NG, HG, S], on=m) for i in range(2)]
        QTB = [sb(f"qtb{i}", [P, NG, P], on=m) for i in range(2)]
        LG = [sb(f"lg{i}", [PARTS * (NH + 1), S], BF16, on=m) for i in range(2)]
        RM = [sb(f"rm{i}", [PARTS * (NH + 1), NH, S], BF16, on=m) for i in range(2)]
        KN = [sb(f"kn{i}", [P, E], on=m) for i in range(2)]
        AUG = [sb(f"aug{i}", [P, NC, NH, DV], on=m) for i in range(2)]
        VW = [sb(f"vw{i}", [P, NH, DV], on=m) for i in range(2)]
        D = [sb(f"d{i}", [P, HG * P], on=m) for i in range(2)]
        C = [sb(f"c{i}", [P, HG * P], on=m) for i in range(2)]
        KVB = [sb(f"kvb{i}", [P, NG, HG, DV], on=m) for i in range(2)]
        TOT = sb("tot", [P, NC * NH, DV], on=m)
        X2N = [sb(f"x2n{i}", [P, NC, E], on=m) for i in range(2)]
        X2T = sb("x2t", [P, NC, NK, P], on=m)
        wabs, wmax, wden, rec, mu, var, z, zp, sc = (
            sb(n, [P, NC * NH], on=m) for n in ("wabs", "wmax", "wden", "rec", "mu", "var", "z_", "zp", "sc"))
        st3 = sb("st3", [P, NC, 6], on=m)
        mv3 = sb("mv3", [P, NC, 2], on=m)
        ve3 = sb("ve3", [P, NC], on=m)
        rs3 = sb("rs3", [P, NC], on=m)
        m.close()
        early.close()

        f = ExitStack()
        w3 = sb("w3", [P, NE, KH, E], on=f)
        r = ExitStack()
        SCN = NT * NE

        def rt(name, w, dt=F32):
            return sb(name, [P, w], dt, on=r)

        m1, m2, first, ex, den2, p1, p2, zer = (
            rt(n, NT) for n in ("m1", "m2", "first", "ex", "den2", "p1", "p2", "zer"))
        ta, tb, oh1, oh2, s2, pw, cum, slotS = (
            rt(n, SCN) for n in ("ta", "tb", "oh1", "oh2", "s2", "pw", "cum", "slotS"))
        abf = rt("abf", SCN, BF16)
        slot, jf, pf = (rt(n, TOPK * NT) for n in ("slot", "jf", "pf"))
        sloti, sj, sp_ = (rt(n, TOPK * NT, I32) for n in ("sloti", "sj", "sp_"))
        nef, base = rt("nef", NE), rt("base", NE + 1)
        nei, neb = rt("nei", NE, I32), rt("neb", NE, I32)
        OHP = [rt(f"ohp{i}", P, BF16) for i in range(2)]
        OHJ = [rt(f"ohj{i}", 2 * TILES, BF16) for i in range(2)]
        inv, ix, fil = rt("inv", 2 * TILES), rt("ix", TILES), rt("fil", TILES)
        efl = [rt(f"efl{i}", TILES) for i in range(2)]
        r.close()
        XG = [sb(f"xg{i}", [P, ROW], on=f) for i in range(NX)]
        XH = [sb(f"xh{i}", [P, NK, P], F32R, on=f) for i in range(2)]
        XL = [sb(f"xl{i}", [P, NK, P], F32R, on=f) for i in range(2)]
        SG = [sb(f"sg{i}", [P, HID], on=f) for i in range(2)]
        HD = [sb(f"hd{i}", [P, HID], on=f) for i in range(2)]
        HT = [sb(f"ht{i}", [P, KH, P], on=f) for i in range(2)]
        YS = [sb(f"ys{i}", [P, E], on=f) for i in range(2)]
        PC = [sb(f"pc{i}", [P, 1], on=f) for i in range(NX)]
        IXG = [sb(f"ixg{i}", [P, 1], U32, on=f) for i in range(NX)]
        IXS = [sb(f"ixs{i}", [P, 1], U32, on=f) for i in range(2)]
        f.close()

        def sems(*names):
            return tuple(sem(n) for n in names)

        def two(name):
            return [sem(f"{name}_{i}") for i in range(2)]

        consts_in, zero_rows, zero_out = sems("consts_in", "zero_rows", "zero_out")
        dve_carrier, pool_carrier = sems("dve_carrier", "pool_carrier")
        in1, qT_out, gate_out = two("in1"), two("qT_out"), two("gate_out")
        ln1_steps, ln1_var, ln1_rstd, q_ready = sems("ln1_steps", "ln1_var", "ln1_rstd", "q_ready")
        qT_psum, qT_ready, gates_psum, gates_ready, gc_ready = sems(
            "qT_psum", "qT_ready", "gates_psum", "gates_ready", "gc_ready")
        pair_in, pair_dve, pair_act, parts_ready, parts_out = sems(
            "pair_in", "pair_dve", "pair_act", "parts_ready", "parts_out")
        abs_ready, log_ready, g_ready, dcol_ready, cols_psum, cols_ready = sems(
            "abs_ready", "log_ready", "g_ready", "dcol_ready", "cols_psum", "cols_ready")
        wst_in = [sem(f"wst_in{i}") for i in range(4)]
        w_hi, w_lo = sems("w_hi", "w_lo")
        in3, inx, x_out, row_out = two("in3"), two("inx"), two("x_out"), two("row_out")
        zeroed, marks_in = sems("zeroed", "marks_in")
        e_ready, d_ready, s_ready, c_ready = sems("e_ready", "d_ready", "s_ready", "c_ready")
        vw_ready, kv_psum, kvb_ready, pv_group, inter_ready = sems(
            "vw_ready", "kv_psum", "kvb_ready", "pv_group", "inter_ready")
        o0_taken, o1_taken, post_steps, cen_ready, sq_ready = sems(
            "o0_taken", "o1_taken", "post_steps", "cen_ready", "sq_ready")
        z_ready, zpow_ready, y_ready, mix_steps, x2_ready, var3, rstd3, x2n_ready = sems(
            "z_ready", "zpow_ready", "y_ready", "mix_steps", "x2_ready", "var3", "rstd3", "x2n_ready")
        x2t_psum, x2t_ready, score_psum, score_ready = sems(
            "x2t_psum", "x2t_ready", "score_psum", "score_ready")
        w3_in, r_steps, r_diff, r_exp, r_ones, r_counts, probs_ready, probs_out = sems(
            "w3_in", "r_steps", "r_diff", "r_exp", "r_ones", "r_counts", "probs_ready", "probs_out")
        onehots, inverted, tables = sems("onehots", "inverted", "tables")
        ixg_ready, ixs_ready, y_added = sems("ixg_ready", "ixs_ready", "y_added")
        xg_in = [sem(f"xg_in_{i}") for i in range(NX)]
        xt_psum, xh_ready, xl_ready, up_ready, sg_ready, hd_ready = sems(
            "xt_psum", "xh_ready", "xl_ready", "up_ready", "sg_ready", "hd_ready")
        ht_psum, ht_ready, y_psum, ys_ready, pc_ready = sems(
            "ht_psum", "ht_ready", "y_psum", "ys_ready", "pc_ready")

        def batches(eng, one):
            one(0, 0)
            one(1, 1)
            with eng.Fori(1, B // 2) as it:
                one(it * 2, 0)
                one(it * 2 + 1, 1)

        def mixing(eng, step):
            step(0, 0, True, False, False)
            step(1, 1, True, True, False)
            with eng.Fori(1, B // 2) as it:
                step(it * 2, 0, True, True, True)
                step(it * 2 + 1, 1, True, True, True)
            step(B, 0, False, True, True)
            step(B + 1, 1, False, False, True)

        def expert_tiles(eng, step):
            for j in range(NX):
                step(j, j)
            with eng.Fori(1, TILES // NX) as it:
                for x in range(NX):
                    step(it * NX + x, x)
            for x in range(NX):
                step(TILES // NX * NX + x, x)

        def stages(j):
            if not isinstance(j, int):
                return True, True, True
            return j < TILES, j + 1 < TILES, j >= 1

        N_CONST = 12
        LOADS3 = 3 + NG * HG + 1 + PARTS + 1

        block = stack.enter_context(nc.Block())

        @block.sync
        def _(sp):
            for dst, src in ((gq, gkq), (gk, gkk), (gv, gkv), (gate_w, gateT)):
                sp.dma_start(dst[:], src.rearrange("p (k g) -> p k g", k=NK)).then_inc(consts_in, 16)
            for dst, src in ((ib, ibias), (fb, fbias), (id_f, ident), (id_b, identb), (mask4, maskT), (io, iota)):
                sp.dma_start(dst[:], src).then_inc(consts_in, 16)
            sp.dma_start(tri[:], trib.rearrange("p (a q) -> p a q", a=2)).then_inc(consts_in, 16)
            sp.dma_start(onwb[:], onw.rearrange("p (h d) -> p h d", h=NH)).then_inc(consts_in, 16)

            def load1(b, i):
                wait(sp, gates_psum, b - 1)
                sp.dma_start(X1[i][:], x_t[b]).then_inc(in1[i], 16)
                sp.dma_start(CT1[i][:], ctxT_t[b]).then_inc(in1[i], 16)
            batches(sp, load1)

            sp.wait_ge(zero_rows, 1)
            sp.dma_start(table[N:ROWS, :], zrow[:]).then_inc(zero_out, 16)
            sp.dma_start(out[N:ROWS, :], zrow[:, 0:E]).then_inc(zero_out, 16)

            for i in range(2):
                sp.wait_ge(gate_out[i], 16 * (B // 2))
            for b in range(B):
                sp.dma_start(gi[b * NH:(b + 1) * NH, :], gate_dram[0:NH, b, :]).then_inc(pair_in, 16)
                sp.dma_start(gf[b * NH:(b + 1) * NH, :], gate_dram[NH:2 * NH, b, :]).then_inc(pair_in, 16)
            sp.wait_ge(parts_ready, 2 * PARTS)
            for k, dst in enumerate((negM_dram, g_dram)):
                sp.dma_start(dst.rearrange("a q s -> q a s"), parts[:, k]).then_inc(parts_out, 16)
            sp.wait_ge(parts_out, 32)
            for i in range(2):
                sp.wait_ge(qT_out[i], 16 * (B // 2))
            sp.wait_ge(zero_out, 32)
            sp.wait_ge(cols_ready, 1)
            sp.wait_ge(zeroed, 1)
            for i in range(2):
                sp.dma_start(LG[i][0:PARTS, :], marks[0:PARTS, 0:S]).then_inc(marks_in, 16)
                sp.dma_start(RM[i][PARTS:PARTS * (NH + 1), :, :],
                             marks[PARTS:PARTS * (NH + 1), :].rearrange("q (h s) -> q h s", h=NH)
                             ).then_inc(marks_in, 16)

            def store(b, i):
                sp.wait_ge(x2n_ready, b + 1)
                sp.dma_start(out_t[b], X[i][:].rearrange("p c h d -> p c (h d)")).then_inc(x_out[i], 16)
                sp.dma_start(table_t[b], X2N[i][:]).then_inc(row_out[i], 16)

            def step(b, i, main, post, route):
                if main:
                    wait(sp, w_lo, 2 * b - 2)
                    for h in range(2):
                        s = 2 * i + h
                        sp.dma_start(wst[s][:], w12T[:, bass.ds((b * 2 + h) * HID, HID)]).then_inc(wst_in[s], 16)
                    wait(sp, inter_ready, b - 1)
                    sp.dma_start(KT[i][:], ctxT_t[b]).then_inc(in3[i], 16)
                    sp.dma_start(AUG[i][:].rearrange("p c h d -> p c (h d)"), ctxv_t[b]).then_inc(in3[i], 16)
                    sp.dma_start(KN[i][:], ctx_t[b, :, 0, :]).then_inc(in3[i], 16)
                    for n in range(NG):
                        for j in range(HG):
                            sp.dma_start(QBD[i][j * DH:(j + 1) * DH, n, j, :],
                                         qT_dram[b, j * DH:(j + 1) * DH, n, :]).then_inc(in3[i], 16)
                    sp.dma_start(QTB[i][:], qT_dram[b, :, :, P:S]).then_inc(in3[i], 16)
                    for q in range(PARTS):
                        sp.dma_start(LG[i][PARTS + q * NH:PARTS + (q + 1) * NH, :],
                                     g_dram[q, bass.ds(b * NH, NH), :]).then_inc(in3[i], 16)
                    sp.dma_start(RM[i][0:PARTS, :, :],
                                 negM_dram[:, bass.ds(b * NH, NH), :]).then_inc(in3[i], 16)
                if route:
                    store(b - 2, i)
                if main:
                    wait(sp, x_out[i], 8 * (b - i))
                    sp.dma_start(X[i][:].rearrange("p c h d -> p c (h d)"), x_t[b]).then_inc(inx[i], 16)
            mixing(sp, step)

            for i in range(2):
                sp.wait_ge(x_out[i], 16 * (B // 2))
                sp.wait_ge(row_out[i], 16 * (B // 2))
            sp.wait_ge(score_ready, B)
            for e in range(NE):
                sp.dma_start(w3[:, e], w3T[:, e * KH * E:(e + 1) * KH * E].rearrange(
                    "p (k d) -> p k d", k=KH)).then_inc(w3_in, 16)
            sp.wait_ge(probs_ready, 1)
            sp.dma_start(table[0:N, E:ROW].rearrange("(t p) e -> p t e", p=P),
                         pw[:].rearrange("p (t e) -> p t e", e=NE)).then_inc(probs_out, 16)
            sp.wait_ge(w3_in, 16 * NE)
            sp.wait_ge(probs_out, 16)

        @block.scalar
        def _(act):
            def stage1(b, i):
                wait(act, qT_psum, b + 1)
                wait(act, gates_psum, b - 1)
                wait(act, qT_out[i], 8 * (b - i))
                nc.scalar.copy(QT1[i][:].rearrange("p k s -> p (k s)"), bank[i][:]).then_inc(qT_ready, 1)
                act.wait_ge(qT_ready, b + 1)
                act.dma_start(qT_dram[b], QT1[i][:]).then_inc(qT_out[i], 16)
                act.wait_ge(gates_psum, b + 1)
                wait(act, gate_out[i], 8 * (b - i))
                nc.scalar.copy(GS1[i][:], bank[2 + i][0:2 * NH, 0:S]).then_inc(gates_ready, 1)
                act.wait_ge(gates_ready, b + 1)
                act.dma_start(gate_dram[:, b, :], GS1[i][:]).then_inc(gate_out[i], 16)
            batches(act, stage1)

            act.wait_ge(pair_in, 16 * 2 * B)
            nc.scalar.activation(fa[:], gf[:], ACT.Abs, bias=fb[:, 0:1]).then_inc(abs_ready, 1)
            act.wait_ge(abs_ready, 1)
            nc.scalar.activation(fe[:], fa[:], ACT.Exp, scale=-1.0).then_inc(pair_act, 1)
            act.wait_ge(pair_act, 1)
            nc.scalar.activation(fl[:], fe[:], ACT.Ln, bias=1.0).then_inc(log_ready, 1)
            act.wait_ge(g_ready, 1)
            nc.scalar.activation(dcol[:, 0, :], g[:, 0:P], ACT.Exp, bias=negM[:, P - 1:P])
            nc.scalar.activation(dcol[:, 1, :], negM[:, P:S], ACT.Exp, bias=M[:, P - 1:P])
            nc.scalar.activation(dcol[:, 2:4, :].rearrange("p a s -> p (a s)"), mx[:], ACT.Exp,
                                 scale=-1.0).then_inc(dcol_ready, 1)

            def step(b, i, main, post, route):
                if post:
                    act.wait_ge(pv_group, 2 * NG * (b - 1) + NG)
                    wait(act, x2_ready, b - 1)
                    nc.scalar.copy(TOT[:, 0:NH, :].rearrange("p h d -> p (h d)"),
                                   bank[4][:, 0:NH * DV]).then_inc(o0_taken, 1)
                for n in range(2 * NG):
                    k = b * 2 * NG + n
                    if main:
                        act.wait_ge(e_ready, k + 1)
                        wait(act, c_ready, k - 1)
                        nc.scalar.activation(D[n % 2][:], bank[n % 2][:], ACT.Exp).then_inc(d_ready, 1)
                    if n == 1 and main:
                        act.wait_ge(kv_psum, b + 1)
                        wait(act, inter_ready, b - 1)
                        for j in range(HG):
                            lo, hi = j * DH, (j + 1) * DH
                            kv = bank[6][lo:hi, 0:NG * HG * DV].rearrange("p (n j d) -> p n j d", n=NG, j=HG)
                            nc.scalar.mul(KVB[i][lo:hi, :, j, :], kv[:, :, j, :], KS).then_inc(kvb_ready, 1)
                    if n == 1 and post:
                        act.wait_ge(cen_ready, b)
                        wait(act, row_out[1 - i], 8 * (b - 1 - (1 - i)))
                        wait(act, x2t_psum, b - 2)
                        nc.scalar.activation(X2N[1 - i][:].rearrange("p c (h d) -> p (c h) d", h=NH),
                                             TOT[:, :, 0:DH], ACT.Square).then_inc(sq_ready, 1)
                if route:
                    act.wait_ge(x2t_psum, b - 1)
                    wait(act, score_psum, b - 2)
                    for c in range(NC):
                        nc.scalar.copy(X2T[:, c].rearrange("p k s -> p (k s)"),
                                       bank[6 + c][:, 0:E]).then_inc(x2t_ready, 1)
                if main:
                    for h in range(2):
                        s = 2 * i + h
                        act.wait_ge(wst_in[s], 8 * (b - i) + 16)
                        nc.scalar.copy(w12h[:].rearrange("p e k h -> p (e k h)")[:, bass.ds((b * 2 + h) * HID, HID)],
                                       wst[s][:]).then_inc(w_hi, 1)
            mixing(act, step)

            act.wait_ge(r_diff, 1)
            nc.scalar.activation(ex[:], first[:], ACT.Exp).then_inc(r_exp, 1)

            def expert(j, x):
                i, o = x % 2, 1 - x % 2
                up, ahead, down = stages(j)
                if ahead:
                    act.wait_ge(xt_psum, j + 2)
                    wait(act, up_ready, j)
                    nc.scalar.copy(XH[o][:].rearrange("p k s -> p (k s)"), bank[4][:, 0:E]).then_inc(xh_ready, 1)
                if up:
                    act.wait_ge(up_ready, j + 1)
                    wait(act, hd_ready, j - 1)
                    nc.scalar.activation(SG[i][:], bank[2 * i][:], ACT.Silu).then_inc(sg_ready, 1)
                if down:
                    act.wait_ge(ht_psum, j)
                    wait(act, y_psum, j - 2)
                    nc.scalar.copy(HT[o][:].rearrange("p k s -> p (k s)"), bank[5][:]).then_inc(ht_ready, 1)
                if ahead:
                    weigh(j + 1, (x + 1) % NX)

            def weigh(j, x):
                act.wait_ge(xg_in[x], (16 // NX) * (j - x) + 16)
                wait(act, ys_ready, j - NX + 1)
                e = act.value_load(etab[0:1, bass.ds(j, 1)], min_val=0, max_val=NE - 1)
                nc.scalar.copy(PC[x][:], XG[x][:, bass.ds(e + E, 1)]).then_inc(pc_ready, 1)

            act.wait_ge(tables, 1)
            act.wait_ge(xt_psum, 1)
            nc.scalar.copy(XH[0][:].rearrange("p k s -> p (k s)"), bank[4][:, 0:E]).then_inc(xh_ready, 1)
            weigh(0, 0)
            expert_tiles(act, expert)

        @block.vector
        def _(dve):
            v = nc.vector
            dve.wait_ge(consts_in, 16 * N_CONST)
            v.memset(zrow[:], 0.0).then_inc(zero_rows, 1)
            v.memset(zeros[:], 0.0).then_inc(pair_dve, 1)
            v.memset(neghalf[:], -0.5).then_inc(pair_dve, 1)
            v.tensor_tensor(gc[:], gk[:], gv[:], ALU.add).then_inc(gc_ready, 1)

            K1 = 2 * NC

            def stage1(b, i):
                st = Steps(dve, ln1_steps, K1 * b)
                dve.wait_ge(in1[i], 16 * (b - i) + 32)
                wait(dve, qT_psum, b - 1)
                for c in range(NC):
                    st.then(v.bn_stats(st1[i][:, c, :], X1[i][:, c, :]))
                for c in range(NC):
                    dve.sem_inc(dve_carrier, 1)
                    st.then(v.bn_aggr(mv1[i][:, c, :], st1[i][:, c, :]))
                assert st.n == K1
                v.tensor_scalar(ve1[i][:], mv1[i][:, :, 1], LN_EPS, None, ALU.add).then_inc(ln1_var, 1)
                dve.wait_ge(ln1_rstd, b + 1)
                for c in range(NC):
                    ins = v.tensor_scalar(Q1[i][:, c, :], X1[i][:, c, :], mv1[i][:, c, 0:1], rs1[i][:, c:c + 1],
                                          ALU.subtract, ALU.mult)
                ins.then_inc(q_ready, 1)
            batches(dve, stage1)

            st = Steps(dve, pair_dve, 2)
            dve.wait_ge(pair_in, 16 * 2 * B)
            dve.wait_ge(pair_dve, 2)
            st.then(v.tensor_scalar(fm[:], gf[:], fb[:, 0:1], 0.0, ALU.add, ALU.min))
            dve.wait_ge(log_ready, 1)
            st.then(v.tensor_tensor(lsg[:], fm[:], fl[:], ALU.subtract))
            st.then(v.tensor_tensor_scan(cs[:], lsg[:], zeros[:], 0.0, ALU.add, ALU.add))
            st.then(v.scalar_tensor_tensor(g[:], gi[:], ib[:, 0:1], cs[:], ALU.add, ALU.subtract))
            st.then(v.tensor_tensor_scan(M[:], g[:], g[:], -3.0e38, ALU.max, ALU.max))
            st.then(v.tensor_scalar(negM[:], M[:], -1.0, None, ALU.mult))
            v.tensor_tensor(mx[:], cs[:], M[:], ALU.add).then_inc(g_ready, 1)
            for k, src in enumerate((negM, g)):
                for q in range(PARTS):
                    v.tensor_copy(parts[:, k, q, :], src[:]).then_inc(parts_ready, 1)
                    dve.wait_ge(parts_ready, k * PARTS + q + 1)
                    if q + 1 < PARTS:
                        st.then(v.tensor_tensor(rest[:, k, q, :], src[:], parts[:, k, q, :], ALU.subtract))
                        src = rest[:, k, q, :]
            dve.wait_ge(cols_psum, 1)
            v.tensor_copy(cols[:].rearrange("p a q -> p (a q)"), bank[0][:]).then_inc(cols_ready, 1)
            dve.wait_ge(cols_ready, 1)
            dve.wait_ge(parts_out, 32)
            for i in range(2):
                dve.wait_ge(qT_out[i], 16 * (B // 2))
            dve.wait_ge(zero_out, 32)
            for i in range(2):
                v.memset(QBD[i][:], 0.0)
                ins = v.memset(KVB[i][:], 0.0)
            ins.then_inc(zeroed, 1)

            K3 = 6 + 3 + 1 + 2 * NC

            def heads(t):
                return t[:].unsqueeze(2).broadcast_to([P, NC * NH, DH])

            def step(b, i, main, post, route):
                pb, o = b - 1, 1 - i
                st = Steps(dve, post_steps, K3 * pb) if post else None
                vals = TOT[:, :, 0:DH]

                def combine(n):
                    k = b * 2 * NG + n
                    dve.wait_ge(s_ready, k + 1)
                    dve.wait_ge(d_ready, k + 1)
                    wait(dve, pv_group, k - 1)
                    v.scalar_tensor_tensor(C[n % 2][:], bank[2 + n % 2][:], KS, D[n % 2][:],
                                           ALU.mult, ALU.mult).then_inc(c_ready, 1)

                if main:
                    combine(0)
                if post:
                    dve.wait_ge(inter_ready, pb + 1)
                    wait(dve, x2_ready, pb)
                    fac = cols[:, 1, bass.ds(pb * NH, NH)].unsqueeze(2).broadcast_to([P, NH, DV])
                    st.then(v.tensor_tensor(TOT[:, NH:, :], bank[7][:, 0:NH * DV].rearrange("p (h d) -> p h d", h=NH),
                                            fac, ALU.mult))
                    v.tensor_tensor(TOT[:, NH:, :], TOT[:, NH:, :],
                                    bank[5][:, 0:NH * DV].rearrange("p (h d) -> p h d", h=NH),
                                    ALU.add).then_inc(o1_taken, 1)
                    dve.wait_ge(o1_taken, pb + 1)
                    dve.wait_ge(o0_taken, pb + 1)
                    sums = TOT[:, :, DH]
                    st.then(v.scalar_tensor_tensor(wabs[:], sums, -1.0, sums, ALU.mult, ALU.max))
                    st.then(v.tensor_tensor(wmax[:].rearrange("p (c h) -> p c h", c=NC),
                                            wabs[:].rearrange("p (c h) -> p c h", c=NC),
                                            cols[:, 2:4, bass.ds(pb * NH, NH)], ALU.max))
                    st.then(v.tensor_scalar(wden[:], wmax[:], NORM_EPS, None, ALU.add))
                    st.then(v.reciprocal(rec[:], wden[:]))
                    st.then(v.tensor_reduce(mu[:], vals, AX.X, ALU.add))
                    v.scalar_tensor_tensor(vals, heads(mu), -1.0 / DH, vals, ALU.mult, ALU.add
                                           ).then_inc(cen_ready, 1)
                if main:
                    combine(1)
                if post:
                    dve.wait_ge(sq_ready, pb + 1)
                    st.then(v.tensor_reduce(var[:], X2N[o][:].rearrange("p c (h d) -> p (c h) d", h=NH), AX.X, ALU.add))
                    st.then(v.scalar_tensor_tensor(z[:], var[:], 1.0 / DH, rec[:], ALU.mult, ALU.mult))
                    st.then(v.tensor_tensor(z[:], z[:], rec[:], ALU.mult))
                    v.tensor_scalar(z[:], z[:], HEAD_EPS, None, ALU.add).then_inc(z_ready, 1)
                if main:
                    combine(2)
                if post:
                    dve.wait_ge(zpow_ready, pb + 1)
                    st.then(v.tensor_tensor(sc[:], rec[:], zp[:], ALU.mult))
                    v.tensor_tensor(vals, vals, heads(sc), ALU.mult).then_inc(y_ready, 1)
                if main:
                    combine(3)
                if route:
                    dve.wait_ge(score_psum, b - 1)
                    v.tensor_copy(scores[:, bass.ds((b - 2) * NC, NC), :],
                                  bank[6][:, 0:NC * NE].rearrange("p (c e) -> p c e", c=NC)).then_inc(score_ready, 1)
                if post:
                    dve.wait_ge(x2_ready, pb + 1)
                    for c in range(NC):
                        st.then(v.bn_stats(st3[:, c, :], X[o][:, c].rearrange("p h d -> p (h d)")))
                    for c in range(NC):
                        dve.sem_inc(dve_carrier, 1)
                        st.then(v.bn_aggr(mv3[:, c, :], st3[:, c, :]))
                    v.tensor_scalar(ve3[:], mv3[:, :, 1], LN_EPS, None, ALU.add).then_inc(var3, 1)
                    dve.wait_ge(rstd3, pb + 1)
                    for c in range(NC):
                        ins = v.tensor_scalar(X2N[o][:, c, :], X[o][:, c].rearrange("p h d -> p (h d)"),
                                              mv3[:, c, 0:1], rs3[:, c:c + 1], ALU.subtract, ALU.mult)
                    ins.then_inc(x2n_ready, 1)
                    assert st.n == K3, st.n
            mixing(dve, step)

            st = Steps(dve, r_steps, 0)

            def te(t):
                return t[:].rearrange("p (t e) -> p t e", e=NE)

            def over_e(t):
                return t[:].unsqueeze(2).broadcast_to([P, NT, NE])

            io_e = io[:, 0:NE].unsqueeze(1).broadcast_to([P, NT, NE])
            dve.wait_ge(score_ready, B)
            for i in range(2):
                dve.wait_ge(x_out[i], 16 * (B // 2))
                dve.wait_ge(row_out[i], 16 * (B // 2))

            def argmax(src, best, onehot):
                st.then(v.tensor_reduce(best[:], src, AX.X, ALU.max))
                st.then(v.tensor_tensor(te(ta), src, over_e(best), ALU.is_equal))
                st.then(v.scalar_tensor_tensor(te(tb), te(ta), float(-NE), io_e, ALU.mult, ALU.add))
                st.then(v.tensor_reduce(first[:], te(tb), AX.X, ALU.min))
                st.then(v.tensor_tensor(te(onehot), te(tb), over_e(first), ALU.is_equal))

            argmax(scores[:], m1, oh1)
            st.then(v.scalar_tensor_tensor(te(s2), te(oh1), -3.0e38, scores[:], ALU.mult, ALU.add))
            argmax(te(s2), m2, oh2)
            v.tensor_tensor(abf[:], oh1[:], oh2[:], ALU.add).then_inc(r_ones, 1)
            st.then(v.memset(zer[:], 0.0))
            v.tensor_tensor(first[:], m2[:], m1[:], ALU.subtract).then_inc(r_diff, 1)
            dve.wait_ge(r_exp, 1)
            st.then(v.tensor_scalar(den2[:], ex[:], 1.0, None, ALU.add))
            st.then(v.reciprocal(p1[:], den2[:]))
            st.then(v.tensor_tensor(p2[:], ex[:], p1[:], ALU.mult))
            st.then(v.tensor_tensor(te(ta), te(oh1), over_e(p1), ALU.mult))
            st.then(v.tensor_tensor(te(tb), te(oh2), over_e(p2), ALU.mult))
            v.tensor_tensor(pw[:], ta[:], tb[:], ALU.add).then_inc(probs_ready, 1)

            dve.wait_ge(r_counts, 1)
            rank = bank[0][:, 0:SCN]
            tot = bank[0][:, SCN:2 * SCN]
            for e in range(NE):
                ins = v.tensor_tensor_scan(te(cum)[:, :, e], tot.rearrange("p (t e) -> p t e", e=NE)[:, :, e], zer[:],
                                           0.0, ALU.add, ALU.add)
            st.then(ins)
            st.then(v.tensor_scalar(nei[:], te(cum)[:, NT - 1, :], float(P - 1), None, ALU.add))
            st.then(v.tensor_scalar(neb[:], nei[:], 7, None, ALU.arith_shift_right))
            st.then(v.tensor_copy(nef[:], neb[:]))
            st.then(v.memset(base[:, 0:1], 0.0))
            st.then(v.tensor_tensor_scan(base[:, 1:], nef[:], zer[:, 0:NE], 0.0, ALU.add, ALU.add))
            st.then(v.tensor_tensor(slotS[:], cum[:], tot, ALU.subtract))
            st.then(v.tensor_tensor(slotS[:], slotS[:], rank, ALU.add))
            st.then(v.scalar_tensor_tensor(te(slotS), base[:, 0:NE].unsqueeze(1).broadcast_to([P, NT, NE]), float(P),
                                           te(slotS), ALU.mult, ALU.add))
            for k, oh in enumerate((oh1, oh2)):
                st.then(v.tensor_tensor(ta[:], oh[:], slotS[:], ALU.mult))
                st.then(v.tensor_reduce(slot[:].rearrange("p (t k) -> p t k", k=TOPK)[:, :, k], te(ta), AX.X, ALU.add))
            st.then(v.tensor_copy(sloti[:], slot[:]))
            v.tensor_scalar(sj[:], sloti[:], 7, None, ALU.arith_shift_right)
            st.then(v.tensor_scalar(sp_[:], sloti[:], P - 1, None, ALU.bitwise_and))
            v.tensor_copy(jf[:], sj[:])
            st.then(v.tensor_copy(pf[:], sp_[:]))
            st.then(v.tensor_scalar(efl[1][:], io[:, 0:TILES], base[:, 1:2], None, ALU.is_ge))
            for e in range(2, NE):
                st.then(v.scalar_tensor_tensor(efl[e % 2][:], io[:, 0:TILES], base[:, e:e + 1], efl[1 - e % 2][:],
                                               ALU.is_ge, ALU.add))
            st.then(v.tensor_copy(etab[:], efl[(NE - 1) % 2][:]))

            def onehot(t, k):
                n = t * TOPK + k
                wait(dve, inverted, n - 1)
                v.tensor_scalar(OHP[k][:], io[:, 0:P], pf[:, bass.ds(n, 1)], None, ALU.is_equal)
                v.tensor_scalar(OHJ[k][:, 0:TILES], io[:, 0:TILES], jf[:, bass.ds(n, 1)], io[:, P:P + 1],
                                ALU.is_equal, ALU.mult)
                v.tensor_scalar(OHJ[k][:, TILES:], io[:, 0:TILES], jf[:, bass.ds(n, 1)], io[:, bass.ds(t + 1, 1)],
                                ALU.is_equal, ALU.mult).then_inc(onehots, 1)
            for k in range(TOPK):
                onehot(0, k)
            with dve.Fori(1, NT) as t:
                for k in range(TOPK):
                    onehot(t, k)
            dve.wait_ge(inverted, TOPK * NT)
            st.then(v.tensor_copy(inv[:], bank[1][:, 0:2 * TILES]))
            v.scalar_tensor_tensor(ix[:], inv[:, TILES:], float(P), inv[:, 0:TILES], ALU.mult, ALU.add)
            st.then(v.tensor_scalar(fil[:], inv[:, TILES:], 0.0, io[:, P + 1:P + 2], ALU.is_equal, ALU.mult))
            st.then(v.tensor_tensor(ix[:], ix[:], fil[:], ALU.add))
            v.tensor_scalar(index[:], ix[:], float(-P), None, ALU.add).then_inc(tables, 1)

            def low(j, i):
                dve.wait_ge(xh_ready, j + 1)
                wait(dve, up_ready, j - 1)
                v.tensor_tensor(XL[i][:].rearrange("p k s -> p (k s)"), bank[4][:, 0:E],
                                XH[i][:].bitcast(F32).rearrange("p k s -> p (k s)"),
                                ALU.subtract).then_inc(xl_ready, 1)

            def expert(j, x):
                i = x % 2
                up, ahead, down = stages(j)
                if ahead:
                    low(j + 1, 1 - i)
                if up:
                    dve.wait_ge(sg_ready, j + 1)
                    wait(dve, ht_psum, j - 1)
                    v.tensor_tensor(HD[i][:], SG[i][:], bank[2 * i + 1][:], ALU.mult).then_inc(hd_ready, 1)
                if down:
                    o = 1 - i
                    dve.wait_ge(y_psum, j)
                    dve.wait_ge(pc_ready, j)
                    wait(dve, y_added, 16 * (j - 2))
                    v.tensor_scalar(YS[o][:], bank[6][:, 0:E], PC[(x - 1) % NX][:, 0:1], None, ALU.mult).then_inc(ys_ready, 1)
            low(0, 0)
            expert_tiles(dve, expert)

        @block.gpsimd
        def _(pool):
            q = nc.gpsimd

            def stage1(b, i):
                pool.wait_ge(ln1_var, b + 1)
                q.tensor_tensor(rs1[i][:], ve1[i][:], neghalf[:, 0:NC], ALU.pow).then_inc(ln1_rstd, 1)
            pool.wait_ge(pair_dve, 2)
            batches(pool, stage1)
            pool.wait_ge(zeroed, 1)

            def step(b, i, main, post, route):
                pb, o = b - 1, 1 - i
                if main:
                    pool.wait_ge(in3[i], 16 * LOADS3 * ((b - i) // 2 + 1) if isinstance(b, int)
                                 else (b - i) * (8 * LOADS3) + 16 * LOADS3)
                    wait(pool, inter_ready, b - 1)
                    q.tensor_tensor(VW[i][:], AUG[i][:, 0],
                                    cols[:, 0, bass.ds(b * NH, NH)].unsqueeze(2).broadcast_to([P, NH, DV]),
                                    ALU.mult).then_inc(vw_ready, 1)

                def low(h):
                    s = 2 * i + h
                    pool.wait_ge(w_hi, 2 * b + h + 1)
                    piece = bass.ds((b * 2 + h) * HID, HID)
                    q.tensor_tensor(w12l[:].rearrange("p e k h -> p (e k h)")[:, piece], wst[s][:],
                                    w12h[:].bitcast(F32).rearrange("p e k h -> p (e k h)")[:, piece],
                                    ALU.subtract).then_inc(w_lo, 1)
                if post:
                    pool.wait_ge(z_ready, pb + 1)
                    q.tensor_tensor(zp[:], z[:], neghalf[:], ALU.pow).then_inc(zpow_ready, 1)
                    pool.wait_ge(y_ready, pb + 1)
                    for c in range(NC):
                        part = TOT[:, c * NH:(c + 1) * NH, 0:DH]
                        q.tensor_tensor(part, part, onwb[:], ALU.mult).then_inc(mix_steps, 1)
                    pool.wait_ge(inx[o], 8 * (pb - o) + 16)
                    for c in range(NC):
                        part = TOT[:, c * NH:(c + 1) * NH, 0:DH]
                        pool.wait_ge(mix_steps, NC * pb + c + 1)
                        ins = q.tensor_tensor(X[o][:, c], X[o][:, c], part, ALU.add)
                    ins.then_inc(x2_ready, 1)
                    pool.wait_ge(var3, pb + 1)
                    q.tensor_tensor(rs3[:], ve3[:], neghalf[:, 0:NC], ALU.pow).then_inc(rstd3, 1)
                if main:
                    low(0)
                    low(1)
            mixing(pool, step)

            def gather(j, x):
                wait(pool, xt_psum, j - NX + 1)
                wait(pool, pc_ready, j - NX + 1)
                pool.sem_inc(pool_carrier, 1)
                q.tensor_copy(IXG[x][:], index[:, bass.ds(j, 1)]).then_inc(ixg_ready, 1)
                pool.wait_ge(ixg_ready, j + 1)
                pool.sem_inc(pool_carrier, 1)
                q.indirect_dma_start(out=XG[x][:], out_offset=None, in_=table,
                                     in_offset=bass.IndirectOffsetOnAxis(ap=IXG[x][:, 0:1], axis=0)
                                     ).then_inc(xg_in[x], 16)

            def add(j, i):
                wait(pool, y_added, 16 * j)
                pool.sem_inc(pool_carrier, 1)
                q.tensor_copy(IXS[i][:], index[:, bass.ds(j, 1)]).then_inc(ixs_ready, 1)
                pool.wait_ge(ixs_ready, j + 1)
                pool.wait_ge(ys_ready, j + 1)
                pool.sem_inc(pool_carrier, 1)
                q.indirect_dma_start(out=out, out_offset=bass.IndirectOffsetOnAxis(ap=IXS[i][:, 0:1], axis=0),
                                     in_=YS[i][:], in_offset=None, compute_op=ALU.add).then_inc(y_added, 16)

            def expert(j, x):
                if not isinstance(j, int) or j + NX - 1 < TILES:
                    gather(j + NX - 1, (x - 1) % NX)
                if stages(j)[2]:
                    add(j - 1, 1 - x % 2)

            pool.wait_ge(tables, 1)
            pool.wait_ge(probs_out, 16)
            for i in range(2):
                pool.wait_ge(x_out[i], 16 * (B // 2))
                pool.wait_ge(row_out[i], 16 * (B // 2))
            pool.wait_ge(zero_out, 32)
            for x in range(NX - 1):
                gather(x, x)
            expert_tiles(pool, expert)
            pool.wait_ge(y_added, 16 * TILES)

        @block.tensor
        def _(pe):
            mm = nc.tensor.matmul
            pe.wait_ge(consts_in, 16 * N_CONST)
            pe.wait_ge(gc_ready, 1)

            def turn(b, i):
                pe.wait_ge(q_ready, b + 1)
                wait(pe, qT_ready, b - 1)
                for k in range(NK):
                    for c in range(NC):
                        ins = nc.tensor.transpose(bank[i][:, k * S + c * P:k * S + (c + 1) * P],
                                                  Q1[i][:, c, k * P:(k + 1) * P], id_f[:])
                ins.then_inc(qT_psum, 1)

            def gates(b, i):
                pe.wait_ge(qT_ready, b + 1)
                wait(pe, gates_ready, b - 1)
                o = bank[2 + i][0:2 * NH, 0:S]
                for k in range(NK):
                    mm(o, gq[:, k, :], QT1[i][:, k, :], start=(k == 0), stop=False)
                for k in range(NK):
                    ins = mm(o, gc[:, k, :], CT1[i][:, k, :], start=False, stop=(k == NK - 1))
                ins.then_inc(gates_psum, 1)

            for i in range(2):
                turn(i, i)
            for i in range(2):
                gates(i, i)
            with pe.Fori(1, B // 2) as it:
                for i in range(2):
                    turn(it * 2 + i, i)
                for i in range(2):
                    gates(it * 2 + i, i)

            pe.wait_ge(dcol_ready, 1)
            for k in range(4):
                ins = nc.tensor.transpose(bank[0][:, k * P:(k + 1) * P], dcol[:, k, :], id_f[:])
            ins.then_inc(cols_psum, 1)
            pe.wait_ge(cols_ready, 1)
            pe.wait_ge(marks_in, 64)

            def step(b, i, main, post, route):
                def exponents(n):
                    c, hg = n // NG, n % NG
                    k = b * 2 * NG + n
                    wait(pe, d_ready, k - 1)
                    mm(bank[n % 2][:], LG[i][:, c * P:(c + 1) * P],
                       RM[i][:, hg * HG:(hg + 1) * HG, c * P:(c + 1) * P], start=True, stop=False)
                    mm(bank[n % 2][:], id_b[:], mask4[:], start=False, stop=True).then_inc(e_ready, 1)
                    wait(pe, c_ready, k - 1)
                    mm(bank[2 + n % 2][:], KT[i][:, hg, c * P:(c + 1) * P],
                       QBD[i][:, hg, :, c * P:(c + 1) * P], start=True, stop=True).then_inc(s_ready, 1)

                def values(n):
                    c, hg = n // NG, n % NG
                    pe.wait_ge(c_ready, b * 2 * NG + n + 1)
                    if n == 0:
                        wait(pe, o0_taken, b)
                    if n == NG:
                        wait(pe, o1_taken, b)
                    for j in range(HG):
                        h = hg * HG + j
                        ins = mm(bank[4 + c][:, h * DV:(h + 1) * DV], C[n % 2][:, j * P:(j + 1) * P],
                                 AUG[i][:, c, h, :], start=True, stop=True)
                    ins.then_inc(pv_group, 1)

                if main:
                    pe.wait_ge(in3[i], 16 * LOADS3 * ((b - i) // 2 + 1) if isinstance(b, int)
                               else (b - i) * (8 * LOADS3) + 16 * LOADS3)
                    exponents(0)
                    exponents(1)
                    pe.wait_ge(vw_ready, b + 1)
                    wait(pe, score_ready, b - 2)
                    for n in range(NG):
                        ins = mm(bank[6][:, n * HG * DV:(n + 1) * HG * DV], KN[i][:, n * P:(n + 1) * P],
                                 VW[i][:, n * HG:(n + 1) * HG, :], start=True, stop=True)
                    ins.then_inc(kv_psum, 1)
                    values(0)
                    exponents(2)
                    values(1)
                    exponents(3)
                if route:
                    rb = b - 2
                    pe.wait_ge(x2n_ready, rb + 1)
                    if main:
                        pe.wait_ge(kvb_ready, HG * (b + 1))
                    else:
                        pe.wait_ge(kvb_ready, HG * B)
                        pe.wait_ge(score_ready, b - 2)
                    pe.wait_ge(o1_taken, b if main else min(b, B))
                    for c in range(NC):
                        for k in range(NK):
                            ins = nc.tensor.transpose(bank[6 + c][:, k * P:(k + 1) * P],
                                                      X2N[i][:, c, k * P:(k + 1) * P], id_f[:])
                    ins.then_inc(x2t_psum, 1)
                if main:
                    values(2)
                    values(3)
                    pe.wait_ge(kvb_ready, HG * (b + 1))
                    wait(pe, o1_taken, b)
                    wait(pe, x2t_ready, NC * (b - 1))
                    for n in range(NG):
                        ins = mm(bank[7][:, n * HG * DV:(n + 1) * HG * DV], QTB[i][:, n, :],
                                 KVB[i][:, n].rearrange("p j d -> p (j d)"), start=True, stop=True)
                    ins.then_inc(inter_ready, 1)
                if route:
                    pe.wait_ge(x2t_ready, NC * (b - 1))
                    for c in range(NC):
                        for k in range(NK):
                            ins = mm(bank[6][:, c * NE:(c + 1) * NE], X2T[:, c, k, :], gate_w[:, k, :],
                                     start=(k == 0), stop=(k == NK - 1))
                    ins.then_inc(score_psum, 1)
            mixing(pe, step)

            pe.wait_ge(r_ones, 1)
            mm(bank[0][:, 0:SCN], tri[:, 0, :], abf[:], start=True, stop=True)
            mm(bank[0][:, SCN:2 * SCN], tri[:, 1, :], abf[:], start=True, stop=True).then_inc(r_counts, 1)

            def invert(n, k, start=False, stop=False):
                pe.wait_ge(onehots, n + 1)
                mm(bank[1][:, 0:2 * TILES], OHP[k][:], OHJ[k][:], start=start, stop=stop).then_inc(inverted, 1)
            for k in range(TOPK):
                invert(k, k, start=(k == 0))
            with pe.Fori(1, NT - 1) as t:
                for k in range(TOPK):
                    invert(t * TOPK + k, k)
            for k in range(TOPK):
                invert((NT - 1) * TOPK + k, k, stop=(k == TOPK - 1))

            def rows(j, x):
                pe.wait_ge(xg_in[x], (16 // NX) * (j - x) + 16)
                wait(pe, xl_ready, j)
                for k in range(NK):
                    ins = nc.tensor.transpose(bank[4][:, k * P:(k + 1) * P], XG[x][:, k * P:(k + 1) * P], id_f[:])
                ins.then_inc(xt_psum, 1)

            def expert(j, x):
                i = x % 2
                up, ahead, down = stages(j)
                if up:
                    e = pe.value_load(etab[0:1, bass.ds(j, 1)], min_val=0, max_val=NE - 1)
                    pe.wait_ge(xl_ready, j + 1)
                    wait(pe, hd_ready, j - 1)
                    for half in range(2):
                        o = bank[2 * i + half][:]
                        for k in range(NK):
                            wh = w12h[:, bass.ds(e, 1), k, half * HID:(half + 1) * HID].rearrange("p a h -> p (a h)")
                            wl = w12l[:, bass.ds(e, 1), k, half * HID:(half + 1) * HID].rearrange("p a h -> p (a h)")
                            mm(o, XH[i][:, k, :], wl, start=(k == 0), stop=False)
                            mm(o, XL[i][:, k, :], wh, start=False, stop=False)
                            ins = mm(o, XH[i][:, k, :], wh, start=False, stop=(k == NK - 1))
                    ins.then_inc(up_ready, 1)
                if ahead:
                    rows(j + 1, (x + 1) % NX)
                if down:
                    o = 1 - i
                    pe.wait_ge(hd_ready, j)
                    wait(pe, ht_ready, j - 1)
                    for k in range(KH):
                        ins = nc.tensor.transpose(bank[5][:, k * P:(k + 1) * P], HD[o][:, k * P:(k + 1) * P], id_f[:])
                    ins.then_inc(ht_psum, 1)
                    ed = pe.value_load(etab[0:1, bass.ds(j - 1, 1)], min_val=0, max_val=NE - 1)
                    pe.wait_ge(ht_ready, j)
                    wait(pe, ys_ready, j - 1)
                    for k in range(KH):
                        ins = mm(bank[6][:, 0:E], HT[o][:, k, :],
                                 w3[:, bass.ds(ed, 1), k, :].rearrange("p a d -> p (a d)"),
                                 start=(k == 0), stop=(k == KH - 1))
                    ins.then_inc(y_psum, 1)

            pe.wait_ge(tables, 1)
            pe.wait_ge(w3_in, 16 * NE)
            rows(0, 0)
            expert_tiles(pe, expert)


_OUT = (ROWS, E)


def kernel(x, ctx_1024, L0_xattn_igate_kernel, L0_xattn_igate_bias, L0_xattn_fgate_kernel,
           L0_xattn_fgate_bias, L0_xattn_outnorm_weight, L0_ffn_w12, L0_ffn_w3, L0_ffn_gate_w):
    import ml_dtypes
    import concourse.bacc as bacc
    from concourse.bass_utils import run_bass_kernel_spmd as run

    bf = ml_dtypes.bfloat16
    a = {k: np.asarray(v) for k, v in dict(
        x=x, ctx=ctx_1024, ik=L0_xattn_igate_kernel, ib=L0_xattn_igate_bias, fk=L0_xattn_fgate_kernel,
        fb=L0_xattn_fgate_bias, onw=L0_xattn_outnorm_weight, w12=L0_ffn_w12, w3=L0_ffn_w3,
        gate=L0_ffn_gate_w).items()}
    ctx2 = a["ctx"].reshape(N, E)
    gk = np.concatenate([a["ik"], a["fk"]], axis=1).reshape(3, NK, P, 2 * NH).transpose(0, 2, 1, 3).reshape(3, P, -1)
    p, q = np.arange(P)[:, None], np.arange(P)[None, :]
    marks = np.ones((PARTS * (NH + 1), NH * S), np.float32)
    marks[PARTS:] = np.tile(np.repeat(np.eye(NH), S, axis=1), (PARTS, 1))
    ins = {
        "x": a["x"].reshape(N, E),
        "ctx": ctx2,
        "ctxv": np.concatenate([ctx2.reshape(N, NH, DH), np.ones((N, NH, 1), np.float32)], axis=2).reshape(N, NH * DV),
        "ctxT": ctx2.T,
        "gkq": gk[0], "gkk": gk[1], "gkv": gk[2],
        "ibias": np.tile(a["ib"], B)[:, None],
        "fbias": np.tile(a["fb"], B)[:, None],
        "onw": np.broadcast_to(a["onw"].reshape(1, E), (P, E)),
        "w12T": a["w12"].transpose(2, 0, 1).reshape(NK, P, NE, 2 * HID).transpose(1, 2, 0, 3).reshape(P, -1),
        "w3T": a["w3"].transpose(2, 0, 1).reshape(KH, P, NE, E).transpose(1, 2, 0, 3).reshape(P, -1),
        "gateT": a["gate"].T.reshape(NK, P, NE).transpose(1, 0, 2).reshape(P, -1),
        "ident": np.eye(P, dtype=np.float32),
        "identb": np.eye(P).astype(bf),
        "maskT": np.tile(np.where(p > q, MASKED, 0.0), (1, HG)).astype(bf),
        "trib": np.concatenate([p < q, np.ones((P, P))], axis=1).astype(bf),
        "marks": marks.astype(bf),
        "iota": np.concatenate([np.broadcast_to(q, (P, P)), p, N + P + p], axis=1).astype(np.float32),
    }
    nc = bacc.Bacc("TRN2", target_bir_lowering=False, num_devices=1)
    arrays, args = {}, []
    for name, v in ins.items():
        arrays["in_" + name] = np.ascontiguousarray(v)
        args.append(nc.dram_tensor("in_" + name, v.shape, mybir.dt.from_np(v.dtype), kind="ExternalInput").ap())
    args.append(nc.dram_tensor("out_rows", _OUT, F32, kind="ExternalOutput").ap())
    build(nc, *args)
    r = run(nc, [arrays], core_ids=[0])
    return r.results[0]["out_rows"][0:N].reshape(B, S, E)
```

```python
from contextlib import ExitStack

import numpy as np

import concourse.bass as bass
from concourse import mybir

ALU = mybir.AluOpType
ACT = mybir.ActivationFunctionType
AX = mybir.AxisListType
F32 = mybir.dt.float32
F32R = mybir.dt.float32r
BF16 = mybir.dt.bfloat16
I32 = mybir.dt.int32
U32 = mybir.dt.uint32

P = 128
B, S, E = 16, 256, 256
NH, DH = 8, 32
NE, HID = 8, 512
TOPK = 2
NC = S // P
NK = E // P
HG = P // DH
NG = NH // HG
DV = DH + 1
N = B * S
NT = N // P
TILES = (N * TOPK + NE * (P - 1)) // P
ROWS = N + P
ROW = E + NE
KH = HID // P
NX = 4
KS = float(DH) ** -0.5
LN_EPS, HEAD_EPS, NORM_EPS = 1e-5, 1e-6, 1e-6
PARTS = 3
MASKED = -1e30


def wait(eng, sem, value):
    if isinstance(value, int) and value <= 0:
        return
    eng.wait_ge(sem, value)


class Steps:

    def __init__(self, eng, sem, base):
        self.eng, self.sem, self.base, self.n = eng, sem, base, 0

    def then(self, ins):
        ins.then_inc(self.sem, 1)
        self.n += 1
        self.eng.wait_ge(self.sem, self.base + self.n)


def build(nc, x, ctx, ctxv, ctxT, gkq, gkk, gkv, ibias, fbias, onw, w12T, w3T, gateT, ident, identb,
          maskT, trib, marks, iota, out):
    qT_dram = nc.dram_tensor("qT_scratch", (B, P, NG, S), F32).ap()
    gate_dram = nc.dram_tensor("gate_scratch", (B, 2 * NH, S), F32).ap()
    negM_dram = nc.dram_tensor("negM_scratch", (PARTS, B * NH, S), BF16).ap()
    g_dram = nc.dram_tensor("g_scratch", (B, PARTS, NH, S), BF16).ap()
    table = nc.dram_tensor("token_table", (ROWS, ROW), F32).ap()

    x_t = x.rearrange("(b c p) e -> b p c e", c=NC, p=P)
    ctx_t = ctx.rearrange("(b c p) e -> b p c e", c=NC, p=P)
    ctxv_t = ctxv.rearrange("(b c p) e -> b p c e", c=NC, p=P)
    ctxT_t = ctxT.rearrange("(k p) (b s) -> b p k s", p=P, s=S)
    out_t = out[0:N, :].rearrange("(b c p) e -> b p c e", c=NC, p=P)
    table_t = table[0:N, 0:E].rearrange("(b c p) e -> b p c e", c=NC, p=P)

    with ExitStack() as stack:
        def sb(name, shape, dt=F32, on=None):
            return (on or stack).enter_context(nc.sbuf_tensor(name, shape, dt))

        def sem(name):
            return stack.enter_context(nc.semaphore(name))

        bank = [stack.enter_context(nc.psum_tensor(f"bank{i}", [P, 512], F32)) for i in range(8)]

        w12h = sb("w12h", [P, NE, NK, 2 * HID], F32R)
        w12l = sb("w12l", [P, NE, NK, 2 * HID], F32R)
        id_f = sb("id_f", [P, P])
        id_b = sb("id_b", [P, P], BF16)
        tri = sb("tri", [P, 2, P], BF16)
        io = sb("io", [P, P + 2])
        gate_w = sb("gate_w", [P, NK, NE])
        scores = sb("scores", [P, NT, NE])
        etab = sb("etab", [P, TILES], I32)
        index = sb("index", [P, TILES], U32)

        early = ExitStack()
        cols = sb("cols", [P, 4, B * NH], on=early)
        eps = sb("eps", [P, 2], on=early)
        onwb = sb("onwb", [P, NH, DH], on=early)
        mask4 = sb("mask4", [P, HG * P], BF16, on=early)
        wst = [sb(f"wst{i}", [P, HID], on=early) for i in range(2)]

        a = ExitStack()
        gq, gk, gv, gc = (sb(n, [P, NK, 2 * NH], on=a) for n in ("gq", "gk", "gv", "gc"))
        ib, fb = (sb(n, [P, 1], on=a) for n in ("ib", "fb"))
        X1 = [sb(f"x1_{i}", [P, NC, E], on=a) for i in range(4)]
        CT1 = [sb(f"ct1_{i}", [P, NK, S], on=a) for i in range(4)]
        Q1 = [sb(f"q1_{i}", [P, NC, E], on=a) for i in range(2)]
        QT1 = [sb(f"qt1_{i}", [P, NK, S], on=a) for i in range(2)]
        GS1 = [sb(f"gs1_{i}", [2 * NH, S], on=a) for i in range(2)]
        st1 = [sb(f"st1_{i}", [P, NC, 6], on=a) for i in range(4)]
        mv1 = [sb(f"mv1_{i}", [P, NC, 2], on=a) for i in range(4)]
        lnv1 = [sb(f"lnv1_{i}", [P, NC], on=a) for i in range(4)]
        rs1 = [sb(f"rs1_{i}", [P, NC], on=a) for i in range(4)]
        gi, gf, fa, fm, fe, fl, lsg, cs, g, M, negM, mx, zeros = (
            sb(n, [P, S], on=a) for n in ("gi", "gf", "fa", "fm", "fe", "fl", "lsg", "cs", "g_", "M_",
                                          "negM", "mx", "zeros"))
        dcol = sb("dcol", [P, 4, P], on=a)
        parts = sb("parts", [P, 2, PARTS, S], BF16, on=a)
        rest = sb("rest", [P, 2, PARTS - 1, S], on=a)
        zrow = sb("zrow", [P, ROW], on=a)
        a.close()

        m = ExitStack()
        X = [sb(f"x3_{i}", [P, NC, NH, DH], on=m) for i in range(2)]
        KT = [sb(f"kt{i}", [P, NG, S], on=m) for i in range(2)]
        QBD = [sb(f"qbd{i}", [P, NG, HG, S], on=m) for i in range(2)]
        QTB = [sb(f"qtb{i}", [P, NG, P], on=m) for i in range(2)]
        LG = [sb(f"lg{i}", [PARTS * (NH + 1), S], BF16, on=m) for i in range(2)]
        RM = [sb(f"rm{i}", [PARTS * (NH + 1), NH, S], BF16, on=m) for i in range(2)]
        KN = [sb(f"kn{i}", [P, E], on=m) for i in range(2)]
        AUG = [sb(f"aug{i}", [P, NC, NH, DV], on=m) for i in range(2)]
        VW = [sb(f"vw{i}", [P, NH, DV], on=m) for i in range(2)]
        D = [sb(f"d{i}", [P, HG * P], on=m) for i in range(2)]
        C = [sb(f"c{i}", [P, HG * P], on=m) for i in range(2)]
        KVB = [sb(f"kvb{i}", [P, NG, HG, DV], on=m) for i in range(2)]
        TOT = [sb(f"tot{i}", [P, NC * NH, DV], on=m) for i in range(2)]
        X2N = [sb(f"x2n{i}", [P, NC, E], on=m) for i in range(2)]
        X2T = sb("x2t", [P, NC * NK, P], on=m)
        wabs, wmax, wden, rec, mu, var, z, z2, lnz, zp, sc = (
            sb(n, [P, NC * NH], on=m)
            for n in ("wabs", "wmax", "wden", "rec", "mu", "var", "z_", "z2_", "lnz", "zp", "sc"))
        st3 = sb("st3", [P, NC, 6], on=m)
        mv3 = sb("mv3", [P, NC, 2], on=m)
        lnv3 = sb("lnv3", [P, NC], on=m)
        rs3 = sb("rs3", [P, NC], on=m)
        m.close()
        early.close()

        f = ExitStack()
        w3 = sb("w3", [P, NE, KH, E], on=f)
        r = ExitStack()
        SCN = NT * NE

        def rt(name, w, dt=F32):
            return sb(name, [P, w], dt, on=r)

        m1, m2, first, ex, den2, p1, p2, zer = (
            rt(n, NT) for n in ("m1", "m2", "first", "ex", "den2", "p1", "p2", "zer"))
        ta, tb, oh1, oh2, s2, pw, cum, slotS = (
            rt(n, SCN) for n in ("ta", "tb", "oh1", "oh2", "s2", "pw", "cum", "slotS"))
        abf = rt("abf", SCN, BF16)
        slot, jf, pf = (rt(n, TOPK * NT) for n in ("slot", "jf", "pf"))
        sloti, sj, sp_ = (rt(n, TOPK * NT, I32) for n in ("sloti", "sj", "sp_"))
        nef, base = rt("nef", NE), rt("base", NE + 1)
        nei, neb = rt("nei", NE, I32), rt("neb", NE, I32)
        OHP = [rt(f"ohp{i}", P, BF16) for i in range(2)]
        OHJ = [rt(f"ohj{i}", 2 * TILES, BF16) for i in range(2)]
        inv, ix, fil = rt("inv", 2 * TILES), rt("ix", TILES), rt("fil", TILES)
        efl = [rt(f"efl{i}", TILES) for i in range(2)]
        r.close()
        XG = [sb(f"xg{i}", [P, ROW], on=f) for i in range(NX)]
        XH = [sb(f"xh{i}", [P, NK, P], F32R, on=f) for i in range(2)]
        XL = [sb(f"xl{i}", [P, NK, P], F32R, on=f) for i in range(2)]
        SG = [sb(f"sg{i}", [P, HID], on=f) for i in range(2)]
        HD = [sb(f"hd{i}", [P, HID], on=f) for i in range(2)]
        HT = [sb(f"ht{i}", [P, KH, P], on=f) for i in range(2)]
        YS = [sb(f"ys{i}", [P, E], on=f) for i in range(2)]
        PC = [sb(f"pc{i}", [P, 1], on=f) for i in range(NX)]
        IXG = [sb(f"ixg{i}", [P, 1], U32, on=f) for i in range(NX)]
        IXS = [sb(f"ixs{i}", [P, 1], U32, on=f) for i in range(2)]
        f.close()

        def sems(*names):
            return tuple(sem(n) for n in names)

        def two(name):
            return [sem(f"{name}_{i}") for i in range(2)]

        consts_in, zero_rows, zero_out = sems("consts_in", "zero_rows", "zero_out")
        dve_carrier, pool_carrier = sems("dve_carrier", "pool_carrier")
        qT_out, gate_out = two("qT_out"), two("gate_out")
        x1_in, ct1_in = ([sem(f"{n}_{i}") for i in range(4)] for n in ("x1_in", "ct1_in"))
        ln1_steps, ln1_log, ln1_rstd, q_ready, eps_set = sems(
            "ln1_steps", "ln1_log", "ln1_rstd", "q_ready", "eps_set")
        qT_psum, qT_ready, gates_psum, gates_ready, gc_ready = sems(
            "qT_psum", "qT_ready", "gates_psum", "gates_ready", "gc_ready")
        pair_in, pair_dve, pair_act, parts_ready, parts_out = sems(
            "pair_in", "pair_dve", "pair_act", "parts_ready", "parts_out")
        abs_ready, log_ready, g_ready, dcol_ready, cols_psum, cols_ready = sems(
            "abs_ready", "log_ready", "g_ready", "dcol_ready", "cols_psum", "cols_ready")
        wst_in = two("wst_in")
        w_hi, w_lo = sems("w_hi", "w_lo")
        in3, inx, x_out, row_out = two("in3"), two("inx"), two("x_out"), two("row_out")
        zeroed, marks_in, y_done = sems("zeroed", "marks_in", "y_done")
        e_ready, d_ready, s_ready, c_ready = sems("e_ready", "d_ready", "s_ready", "c_ready")
        vw_ready, kv_psum, kvb_ready, pv_group, inter_ready = sems(
            "vw_ready", "kv_psum", "kvb_ready", "pv_group", "inter_ready")
        o0_taken, o1_taken, post_steps, cen_ready, sq_ready = sems(
            "o0_taken", "o1_taken", "post_steps", "cen_ready", "sq_ready")
        z_ready, z_log, zpow_ready, sc_ready, mix_steps, x2_ready = sems(
            "z_ready", "z_log", "zpow_ready", "sc_ready", "mix_steps", "x2_ready")
        late_steps, var3_log, rstd3, x2n_ready = sems("late_steps", "var3_log", "rstd3", "x2n_ready")
        x2t_psum, x2t_ready, score_psum, score_ready = sems(
            "x2t_psum", "x2t_ready", "score_psum", "score_ready")
        w3_in, r_steps, r_diff, r_exp, r_ones, r_counts, probs_ready, probs_out = sems(
            "w3_in", "r_steps", "r_diff", "r_exp", "r_ones", "r_counts", "probs_ready", "probs_out")
        onehots, inverted, tables = sems("onehots", "inverted", "tables")
        ixg_ready, ixs_ready, y_added = sems("ixg_ready", "ixs_ready", "y_added")
        xg_in = [sem(f"xg_in_{i}") for i in range(NX)]
        xt_psum, xh_ready, xl_ready, up_ready, sg_ready, hd_ready = sems(
            "xt_psum", "xh_ready", "xl_ready", "up_ready", "sg_ready", "hd_ready")
        ht_psum, ht_ready, y_psum, ys_ready, pc_ready = sems(
            "ht_psum", "ht_ready", "y_psum", "ys_ready", "pc_ready")

        def gating(eng, step):
            for b in range(4):
                step(b, b)
            with eng.Fori(1, B // 4) as it:
                for x in range(4):
                    step(it * 4 + x, x)
            for b in range(B, B + 2):
                step(b, b % 4)

        def mixing(eng, step):
            for b in range(4):
                step(b, b % 2)
            with eng.Fori(2, B // 2) as it:
                step(it * 2, 0)
                step(it * 2 + 1, 1)
            for b in range(B, B + 3):
                step(b, b % 2)

        def has(b, back):
            return not isinstance(b, int) or 0 <= b - back < B

        def expert_tiles(eng, step):
            for j in range(NX):
                step(j, j)
            with eng.Fori(1, TILES // NX) as it:
                for x in range(NX):
                    step(it * NX + x, x)
            for x in range(NX):
                step(TILES // NX * NX + x, x)

        def stages(j):
            if not isinstance(j, int):
                return True, True, True
            return j < TILES, j + 1 < TILES, j >= 1

        N_CONST = 12
        K1 = 2 * NC
        LOADS3 = 3 + HG + 3

        block = stack.enter_context(nc.Block())

        @block.sync
        def _(sp):
            for dst, src in ((gq, gkq), (gk, gkk), (gv, gkv), (gate_w, gateT)):
                sp.dma_start(dst[:], src.rearrange("p (k g) -> p k g", k=NK)).then_inc(consts_in, 16)
            for dst, src in ((ib, ibias), (fb, fbias), (id_f, ident), (id_b, identb), (mask4, maskT), (io, iota)):
                sp.dma_start(dst[:], src).then_inc(consts_in, 16)
            sp.dma_start(tri[:], trib.rearrange("p (a q) -> p a q", a=2)).then_inc(consts_in, 16)
            sp.dma_start(onwb[:], onw.rearrange("p (h d) -> p h d", h=NH)).then_inc(consts_in, 16)

            def load_w(piece, i):
                wait(sp, w_lo, piece - 1)
                sp.dma_start(wst[i][:], w12T[:, bass.ds(piece * HID, HID)]).then_inc(wst_in[i], 16)

            def load1(b, x):
                if has(b, 0):
                    wait(sp, q_ready, b - 3)
                    sp.dma_start(X1[x][:], x_t[b]).then_inc(x1_in[x], 16)
                    wait(sp, gates_psum, b - 3)
                    sp.dma_start(CT1[x][:], ctxT_t[b]).then_inc(ct1_in[x], 16)
                    load_w(b, x % 2)
            gating(sp, load1)

            sp.wait_ge(zero_rows, 1)
            sp.dma_start(table[N:ROWS, :], zrow[:]).then_inc(zero_out, 16)
            sp.dma_start(out[N:ROWS, :], zrow[:, 0:E]).then_inc(zero_out, 16)

            for i in range(2):
                sp.wait_ge(gate_out[i], 16 * (B // 2))
            for k, dst in enumerate((gi, gf)):
                sp.dma_start(dst[:], gate_dram[:, k * NH:(k + 1) * NH, :]).then_inc(pair_in, 16)
            sp.wait_ge(parts_ready, 2 * PARTS)
            sp.dma_start(negM_dram.rearrange("a q s -> q a s"), parts[:, 0]).then_inc(parts_out, 16)
            for q in range(PARTS):
                sp.dma_start(g_dram[:, q], parts[:, 1, q, :]).then_inc(parts_out, 16)
            sp.wait_ge(parts_out, 16 * (1 + PARTS))
            for i in range(2):
                sp.wait_ge(qT_out[i], 16 * (B // 2))
            sp.wait_ge(zero_out, 32)
            sp.wait_ge(cols_ready, 1)
            sp.wait_ge(zeroed, 1)
            for i in range(2):
                sp.dma_start(LG[i][0:PARTS, :], marks[0:PARTS, 0:S]).then_inc(marks_in, 16)
                sp.dma_start(RM[i][PARTS:PARTS * (NH + 1), :, :],
                             marks[PARTS:PARTS * (NH + 1), :].rearrange("q (h s) -> q h s", h=NH)
                             ).then_inc(marks_in, 16)

            def store(b, i):
                sp.wait_ge(x2n_ready, b + 1)
                sp.dma_start(out_t[b], X[i][:].rearrange("p c h d -> p c (h d)")).then_inc(x_out[i], 16)
                sp.dma_start(table_t[b], X2N[i][:]).then_inc(row_out[i], 16)

            def step(b, i):
                o = 1 - i
                if has(b, 0):
                    wait(sp, inter_ready, b - 1)
                    sp.dma_start(KT[i][:], ctxT_t[b]).then_inc(in3[i], 16)
                    sp.dma_start(AUG[i][:].rearrange("p c h d -> p c (h d)"), ctxv_t[b]).then_inc(in3[i], 16)
                    sp.dma_start(KN[i][:], ctx_t[b, :, 0, :]).then_inc(in3[i], 16)
                    for j in range(HG):
                        sp.dma_start(QBD[i][j * DH:(j + 1) * DH, :, j, :],
                                     qT_dram[b, j * DH:(j + 1) * DH]).then_inc(in3[i], 16)
                    sp.dma_start(QTB[i][:], qT_dram[b, :, :, P:S]).then_inc(in3[i], 16)
                    sp.dma_start(LG[i][PARTS:, :], g_dram[b].rearrange("q h s -> (q h) s")).then_inc(in3[i], 16)
                    sp.dma_start(RM[i][0:PARTS, :, :],
                                 negM_dram[:, bass.ds(b * NH, NH), :]).then_inc(in3[i], 16)
                if has(b, 3):
                    store(b - 3, o)
                if has(b, 1):
                    wait(sp, x_out[o], 8 * (b - 1 - o))
                    sp.dma_start(X[o][:].rearrange("p c h d -> p c (h d)"), x_t[b - 1]).then_inc(inx[o], 16)
                if has(b, 0):
                    load_w(b + B, i)
            mixing(sp, step)

            for i in range(2):
                sp.wait_ge(x_out[i], 16 * (B // 2))
                sp.wait_ge(row_out[i], 16 * (B // 2))
            sp.wait_ge(score_ready, B)
            for e in range(NE):
                sp.dma_start(w3[:, e], w3T[:, e * KH * E:(e + 1) * KH * E].rearrange(
                    "p (k d) -> p k d", k=KH)).then_inc(w3_in, 16)
            sp.wait_ge(probs_ready, 1)
            sp.dma_start(table[0:N, E:ROW].rearrange("(t p) e -> p t e", p=P),
                         pw[:].rearrange("p (t e) -> p t e", e=NE)).then_inc(probs_out, 16)
            sp.wait_ge(w3_in, 16 * NE)
            sp.wait_ge(probs_out, 16)

        @block.scalar
        def _(act):
            def power(out_, log_, in_, column, counter, n, ready):
                nc.scalar.activation(log_, in_, ACT.Ln, bias=eps[:, column:column + 1]).then_inc(counter, 1)
                act.wait_ge(counter, n)
                nc.scalar.activation(out_, log_, ACT.Exp, scale=-0.5).then_inc(ready, 1)

            def high(piece, i, count):
                act.wait_ge(wst_in[i], count)
                nc.scalar.copy(w12h[:].rearrange("p e k h -> p (e k h)")[:, bass.ds(piece * HID, HID)],
                               wst[i][:]).then_inc(w_hi, 1)

            def stage1(b, x):
                i, o = x % 2, 1 - x % 2
                if has(b, 0):
                    act.wait_ge(ln1_steps, K1 * (b + 1))
                    power(rs1[x][:], lnv1[x][:], mv1[x][:, :, 1], 0, ln1_log, b + 1, ln1_rstd)
                if has(b, 1):
                    a_ = b - 1
                    act.wait_ge(qT_psum, a_ + 1)
                    wait(act, gates_psum, a_ - 1)
                    wait(act, qT_out[o], 8 * (a_ - o))
                    nc.scalar.copy(QT1[o][:].rearrange("p k s -> p (k s)"), bank[o][:]).then_inc(qT_ready, 1)
                    act.wait_ge(qT_ready, a_ + 1)
                    act.dma_start(qT_dram[a_], QT1[o][:]).then_inc(qT_out[o], 16)
                if has(b, 2):
                    a_ = b - 2
                    act.wait_ge(gates_psum, a_ + 1)
                    wait(act, gate_out[i], 8 * (a_ - i))
                    nc.scalar.copy(GS1[i][:], bank[2 + i][0:2 * NH, 0:S]).then_inc(gates_ready, 1)
                    act.wait_ge(gates_ready, a_ + 1)
                    act.dma_start(gate_dram[a_], GS1[i][:]).then_inc(gate_out[i], 16)
                if has(b, 0):
                    high(b, i, 8 * (b - i) + 16)
            nc.scalar.preload_act_table_set("natural_log_exp_and_others")
            act.wait_ge(eps_set, 1)
            gating(act, stage1)

            act.wait_ge(pair_in, 32)
            nc.scalar.activation(fa[:], gf[:], ACT.Abs, bias=fb[:, 0:1]).then_inc(abs_ready, 1)
            act.wait_ge(abs_ready, 1)
            nc.scalar.activation(fe[:], fa[:], ACT.Exp, scale=-1.0).then_inc(pair_act, 1)
            act.wait_ge(pair_act, 1)
            nc.scalar.activation(fl[:], fe[:], ACT.Ln, bias=1.0).then_inc(log_ready, 1)
            act.wait_ge(g_ready, 1)
            nc.scalar.activation(dcol[:, 0, :], g[:, 0:P], ACT.Exp, bias=negM[:, P - 1:P])
            nc.scalar.activation(dcol[:, 1, :], negM[:, P:S], ACT.Exp, bias=M[:, P - 1:P])
            nc.scalar.activation(dcol[:, 2:4, :].rearrange("p a s -> p (a s)"), mx[:], ACT.Exp,
                                 scale=-1.0).then_inc(dcol_ready, 1)

            def step(b, i):
                o = 1 - i
                if has(b, 1):
                    act.wait_ge(pv_group, 2 * NG * (b - 1) + NG)
                    wait(act, x2_ready, b - 2)
                    nc.scalar.copy(TOT[o][:, 0:NH, :].rearrange("p h d -> p (h d)"),
                                   bank[4][:, 0:NH * DV]).then_inc(o0_taken, 1)

                def weights(n):
                    if has(b, 0):
                        k = b * 2 * NG + n
                        act.wait_ge(e_ready, k + 1)
                        wait(act, c_ready, k - 1)
                        nc.scalar.activation(D[n % 2][:], bank[n % 2][:], ACT.Exp).then_inc(d_ready, 1)

                weights(0)
                weights(1)
                if has(b, 0):
                    act.wait_ge(kv_psum, b + 1)
                    wait(act, inter_ready, b - 1)
                    for j in range(HG):
                        lo, hi = j * DH, (j + 1) * DH
                        kv = bank[6][lo:hi, 0:NG * HG * DV].rearrange("p (n j d) -> p n j d", n=NG, j=HG)
                        nc.scalar.mul(KVB[i][lo:hi, :, j, :], kv[:, :, j, :], KS).then_inc(kvb_ready, 1)
                weights(2)
                if has(b, 1):
                    act.wait_ge(cen_ready, b)
                    wait(act, row_out[o], 8 * (b - 1 - o))
                    wait(act, x2t_psum, b - 2)
                    nc.scalar.activation(X2N[o][:].rearrange("p c (h d) -> p (c h) d", h=NH),
                                         TOT[o][:, :, 0:DH], ACT.Square).then_inc(sq_ready, 1)
                if has(b, 3):
                    act.wait_ge(x2t_psum, b - 2)
                    wait(act, score_psum, b - 3)
                    nc.scalar.copy(X2T[:].rearrange("p k s -> p (k s)"), bank[7][:]).then_inc(x2t_ready, 1)
                weights(3)
                if has(b, 2):
                    act.wait_ge(late_steps, 2 * NC * (b - 1))
                    power(rs3[:], lnv3[:], mv3[:, :, 1], 0, var3_log, b - 1, rstd3)
                if has(b, 1):
                    act.wait_ge(z_ready, b)
                    power(zp[:], lnz[:], z2[:], 1, z_log, b, zpow_ready)
                if has(b, 0):
                    high(b + B, i, 8 * (b - i) + 16 + 16 * (B // 2))
            mixing(act, step)

            act.wait_ge(r_diff, 1)
            nc.scalar.activation(ex[:], first[:], ACT.Exp).then_inc(r_exp, 1)

            def expert(j, x):
                i, o = x % 2, 1 - x % 2
                up, ahead, down = stages(j)
                if down:
                    act.wait_ge(ht_psum, j)
                    wait(act, y_psum, j - 2)
                    nc.scalar.copy(HT[o][:].rearrange("p k s -> p (k s)"), bank[5][:]).then_inc(ht_ready, 1)
                if up:
                    act.wait_ge(up_ready, 2 * j + 1)
                    wait(act, hd_ready, j - 1)
                    nc.scalar.activation(SG[i][:], bank[2 * i][:], ACT.Silu).then_inc(sg_ready, 1)
                if ahead:
                    act.wait_ge(xt_psum, j + 2)
                    wait(act, up_ready, 2 * j)
                    nc.scalar.copy(XH[o][:].rearrange("p k s -> p (k s)"), bank[4][:, 0:E]).then_inc(xh_ready, 1)
                if ahead:
                    weigh(j + 1, (x + 1) % NX)

            def weigh(j, x):
                act.wait_ge(xg_in[x], (16 // NX) * (j - x) + 16)
                wait(act, ys_ready, j - NX + 1)
                e = act.value_load(etab[0:1, bass.ds(j, 1)], min_val=0, max_val=NE - 1)
                nc.scalar.copy(PC[x][:], XG[x][:, bass.ds(e + E, 1)]).then_inc(pc_ready, 1)

            act.wait_ge(tables, 1)
            act.wait_ge(xt_psum, 1)
            nc.scalar.copy(XH[0][:].rearrange("p k s -> p (k s)"), bank[4][:, 0:E]).then_inc(xh_ready, 1)
            weigh(0, 0)
            expert_tiles(act, expert)

        @block.vector
        def _(dve):
            v = nc.vector
            dve.wait_ge(consts_in, 16 * N_CONST)
            v.memset(zrow[:], 0.0).then_inc(zero_rows, 1)
            v.memset(zeros[:], 0.0).then_inc(pair_dve, 1)
            v.memset(eps[:, 0:1], LN_EPS)
            v.memset(eps[:, 1:2], HEAD_EPS).then_inc(eps_set, 1)
            v.tensor_tensor(gc[:], gk[:], gv[:], ALU.add).then_inc(gc_ready, 1)

            def stage1(b, x):
                if has(b, 0):
                    st = Steps(dve, ln1_steps, K1 * b)
                    dve.wait_ge(x1_in[x], 4 * (b - x) + 16)
                    for c in range(NC):
                        st.then(v.bn_stats(st1[x][:, c, :], X1[x][:, c, :]))
                    for c in range(NC):
                        dve.sem_inc(dve_carrier, 1)
                        st.then(v.bn_aggr(mv1[x][:, c, :], st1[x][:, c, :]))
                    assert st.n == K1
                if has(b, 1):
                    a_, y, o = b - 1, (x - 1) % 4, 1 - x % 2
                    dve.wait_ge(ln1_rstd, a_ + 1)
                    wait(dve, qT_psum, a_ - 1)
                    for c in range(NC):
                        ins = v.tensor_scalar(Q1[o][:, c, :], X1[y][:, c, :], mv1[y][:, c, 0:1],
                                              rs1[y][:, c:c + 1], ALU.subtract, ALU.mult)
                    ins.then_inc(q_ready, 1)
            gating(dve, stage1)

            st = Steps(dve, pair_dve, 1)
            dve.wait_ge(pair_in, 32)
            dve.wait_ge(pair_dve, 1)
            st.then(v.tensor_scalar(fm[:], gf[:], fb[:, 0:1], 0.0, ALU.add, ALU.min))
            dve.wait_ge(log_ready, 1)
            st.then(v.tensor_tensor(lsg[:], fm[:], fl[:], ALU.subtract))
            st.then(v.tensor_tensor_scan(cs[:], lsg[:], zeros[:], 0.0, ALU.add, ALU.add))
            st.then(v.scalar_tensor_tensor(g[:], gi[:], ib[:, 0:1], cs[:], ALU.add, ALU.subtract))
            st.then(v.tensor_tensor_scan(M[:], g[:], g[:], -3.0e38, ALU.max, ALU.max))
            st.then(v.tensor_scalar(negM[:], M[:], -1.0, None, ALU.mult))
            v.tensor_tensor(mx[:], cs[:], M[:], ALU.add).then_inc(g_ready, 1)
            for k, src in enumerate((negM, g)):
                for q in range(PARTS):
                    v.tensor_copy(parts[:, k, q, :], src[:]).then_inc(parts_ready, 1)
                    dve.wait_ge(parts_ready, k * PARTS + q + 1)
                    if q + 1 < PARTS:
                        st.then(v.tensor_tensor(rest[:, k, q, :], src[:], parts[:, k, q, :], ALU.subtract))
                        src = rest[:, k, q, :]
            dve.wait_ge(cols_psum, 1)
            v.tensor_copy(cols[:].rearrange("p a q -> p (a q)"), bank[0][:]).then_inc(cols_ready, 1)
            dve.wait_ge(cols_ready, 1)
            dve.wait_ge(parts_out, 16 * (1 + PARTS))
            for i in range(2):
                dve.wait_ge(qT_out[i], 16 * (B // 2))
            dve.wait_ge(zero_out, 32)
            for i in range(2):
                v.memset(QBD[i][:], 0.0)
                ins = v.memset(KVB[i][:], 0.0)
            ins.then_inc(zeroed, 1)

            K3 = 7

            def heads(t):
                return t[:].unsqueeze(2).broadcast_to([P, NC * NH, DH])

            def step(b, i):
                pb, lb, o = b - 1, b - 2, 1 - i
                main, post, late = has(b, 0), has(b, 1), has(b, 2)
                st = Steps(dve, post_steps, K3 * pb)
                tot_ = TOT[o]
                vals = tot_[:, :, 0:DH]

                def combine(n):
                    if main:
                        k = b * 2 * NG + n
                        dve.wait_ge(s_ready, k + 1)
                        dve.wait_ge(d_ready, k + 1)
                        wait(dve, pv_group, k - 1)
                        v.scalar_tensor_tensor(C[n % 2][:], bank[2 + n % 2][:], KS, D[n % 2][:],
                                               ALU.mult, ALU.mult).then_inc(c_ready, 1)

                combine(0)
                if post:
                    dve.wait_ge(inter_ready, pb + 1)
                    wait(dve, x2_ready, pb - 1)
                    fac = cols[:, 1, bass.ds(pb * NH, NH)].unsqueeze(2).broadcast_to([P, NH, DV])
                    st.then(v.tensor_tensor(tot_[:, NH:, :], bank[7][:, 0:NH * DV].rearrange("p (h d) -> p h d", h=NH),
                                            fac, ALU.mult))
                    v.tensor_tensor(tot_[:, NH:, :], tot_[:, NH:, :],
                                    bank[5][:, 0:NH * DV].rearrange("p (h d) -> p h d", h=NH),
                                    ALU.add).then_inc(o1_taken, 1)
                combine(1)
                if post:
                    dve.wait_ge(o1_taken, pb + 1)
                    dve.wait_ge(o0_taken, pb + 1)
                    sums = tot_[:, :, DH]
                    st.then(v.scalar_tensor_tensor(wabs[:], sums, -1.0, sums, ALU.mult, ALU.max))
                    st.then(v.tensor_tensor(wmax[:].rearrange("p (c h) -> p c h", c=NC),
                                            wabs[:].rearrange("p (c h) -> p c h", c=NC),
                                            cols[:, 2:4, bass.ds(pb * NH, NH)], ALU.max))
                    st.then(v.tensor_scalar(wden[:], wmax[:], NORM_EPS, None, ALU.add))
                    v.reciprocal(rec[:], wden[:])
                    st.then(v.tensor_reduce(mu[:], vals, AX.X, ALU.add))
                    v.scalar_tensor_tensor(vals, heads(mu), -1.0 / DH, vals, ALU.mult, ALU.add
                                           ).then_inc(cen_ready, 1)
                combine(2)
                if late:
                    sl = Steps(dve, late_steps, 2 * NC * lb)
                    dve.wait_ge(x2_ready, lb + 1)
                    v.bn_stats(st3[:, 0, :], X[i][:, 0].rearrange("p h d -> p (h d)")).then_inc(late_steps, 1)
                    sl.n += 1
                    for c in range(1, NC):
                        sl.then(v.bn_stats(st3[:, c, :], X[i][:, c].rearrange("p h d -> p (h d)")))
                    for c in range(NC):
                        dve.sem_inc(dve_carrier, 1)
                        v.bn_aggr(mv3[:, c, :], st3[:, c, :]).then_inc(late_steps, 1)
                if post:
                    dve.wait_ge(sq_ready, pb + 1)
                    st.then(v.tensor_reduce(var[:], X2N[o][:].rearrange("p c (h d) -> p (c h) d", h=NH), AX.X, ALU.add))
                    st.then(v.scalar_tensor_tensor(z[:], var[:], 1.0 / DH, rec[:], ALU.mult, ALU.mult))
                    v.tensor_tensor(z2[:], z[:], rec[:], ALU.mult).then_inc(z_ready, 1)
                combine(3)
                if late:
                    dve.wait_ge(rstd3, lb + 1)
                    wait(dve, row_out[i], 8 * (lb - i))
                    for c in range(NC):
                        ins = v.tensor_scalar(X2N[i][:, c, :], X[i][:, c].rearrange("p h d -> p (h d)"),
                                              mv3[:, c, 0:1], rs3[:, c:c + 1], ALU.subtract, ALU.mult)
                    ins.then_inc(x2n_ready, 1)
                if post:
                    dve.wait_ge(zpow_ready, pb + 1)
                    wait(dve, y_done, pb)
                    v.tensor_tensor(sc[:], rec[:], zp[:], ALU.mult).then_inc(sc_ready, 1)
                    assert st.n == K3, st.n
                if has(b, 3):
                    dve.wait_ge(score_psum, b - 2)
                    v.tensor_copy(scores[:, bass.ds((b - 3) * NC, NC), :],
                                  bank[6][:, NH * DV:NH * DV + NC * NE].rearrange("p (c e) -> p c e", c=NC)
                                  ).then_inc(score_ready, 1)
            mixing(dve, step)

            st = Steps(dve, r_steps, 0)

            def te(t):
                return t[:].rearrange("p (t e) -> p t e", e=NE)

            def over_e(t):
                return t[:].unsqueeze(2).broadcast_to([P, NT, NE])

            io_e = io[:, 0:NE].unsqueeze(1).broadcast_to([P, NT, NE])
            dve.wait_ge(score_ready, B)
            for i in range(2):
                dve.wait_ge(x_out[i], 16 * (B // 2))
                dve.wait_ge(row_out[i], 16 * (B // 2))

            def argmax(src, best, onehot):
                st.then(v.tensor_reduce(best[:], src, AX.X, ALU.max))
                st.then(v.tensor_tensor(te(ta), src, over_e(best), ALU.is_equal))
                st.then(v.scalar_tensor_tensor(te(tb), te(ta), float(-NE), io_e, ALU.mult, ALU.add))
                st.then(v.tensor_reduce(first[:], te(tb), AX.X, ALU.min))
                st.then(v.tensor_tensor(te(onehot), te(tb), over_e(first), ALU.is_equal))

            argmax(scores[:], m1, oh1)
            st.then(v.scalar_tensor_tensor(te(s2), te(oh1), -3.0e38, scores[:], ALU.mult, ALU.add))
            argmax(te(s2), m2, oh2)
            v.tensor_tensor(abf[:], oh1[:], oh2[:], ALU.add).then_inc(r_ones, 1)
            st.then(v.memset(zer[:], 0.0))
            v.tensor_tensor(first[:], m2[:], m1[:], ALU.subtract).then_inc(r_diff, 1)
            dve.wait_ge(r_exp, 1)
            st.then(v.tensor_scalar(den2[:], ex[:], 1.0, None, ALU.add))
            st.then(v.reciprocal(p1[:], den2[:]))
            st.then(v.tensor_tensor(p2[:], ex[:], p1[:], ALU.mult))
            st.then(v.tensor_tensor(te(ta), te(oh1), over_e(p1), ALU.mult))
            st.then(v.tensor_tensor(te(tb), te(oh2), over_e(p2), ALU.mult))
            v.tensor_tensor(pw[:], ta[:], tb[:], ALU.add).then_inc(probs_ready, 1)

            dve.wait_ge(r_counts, 1)
            rank = bank[0][:, 0:SCN]
            tot = bank[0][:, SCN:2 * SCN]
            for e in range(NE):
                ins = v.tensor_tensor_scan(te(cum)[:, :, e], tot.rearrange("p (t e) -> p t e", e=NE)[:, :, e], zer[:],
                                           0.0, ALU.add, ALU.add)
            st.then(ins)
            st.then(v.tensor_scalar(nei[:], te(cum)[:, NT - 1, :], float(P - 1), None, ALU.add))
            st.then(v.tensor_scalar(neb[:], nei[:], 7, None, ALU.arith_shift_right))
            st.then(v.tensor_copy(nef[:], neb[:]))
            st.then(v.memset(base[:, 0:1], 0.0))
            st.then(v.tensor_tensor_scan(base[:, 1:], nef[:], zer[:, 0:NE], 0.0, ALU.add, ALU.add))
            st.then(v.tensor_tensor(slotS[:], cum[:], tot, ALU.subtract))
            st.then(v.tensor_tensor(slotS[:], slotS[:], rank, ALU.add))
            st.then(v.scalar_tensor_tensor(te(slotS), base[:, 0:NE].unsqueeze(1).broadcast_to([P, NT, NE]), float(P),
                                           te(slotS), ALU.mult, ALU.add))
            for k, oh in enumerate((oh1, oh2)):
                st.then(v.tensor_tensor(ta[:], oh[:], slotS[:], ALU.mult))
                st.then(v.tensor_reduce(slot[:].rearrange("p (t k) -> p t k", k=TOPK)[:, :, k], te(ta), AX.X, ALU.add))
            st.then(v.tensor_copy(sloti[:], slot[:]))
            v.tensor_scalar(sj[:], sloti[:], 7, None, ALU.arith_shift_right)
            st.then(v.tensor_scalar(sp_[:], sloti[:], P - 1, None, ALU.bitwise_and))
            v.tensor_copy(jf[:], sj[:])
            st.then(v.tensor_copy(pf[:], sp_[:]))
            st.then(v.tensor_scalar(efl[1][:], io[:, 0:TILES], base[:, 1:2], None, ALU.is_ge))
            for e in range(2, NE):
                st.then(v.scalar_tensor_tensor(efl[e % 2][:], io[:, 0:TILES], base[:, e:e + 1], efl[1 - e % 2][:],
                                               ALU.is_ge, ALU.add))
            st.then(v.tensor_copy(etab[:], efl[(NE - 1) % 2][:]))

            def onehot(t, k):
                n = t * TOPK + k
                wait(dve, inverted, n - 1)
                v.tensor_scalar(OHP[k][:], io[:, 0:P], pf[:, bass.ds(n, 1)], None, ALU.is_equal)
                v.tensor_scalar(OHJ[k][:, 0:TILES], io[:, 0:TILES], jf[:, bass.ds(n, 1)], io[:, P:P + 1],
                                ALU.is_equal, ALU.mult)
                v.tensor_scalar(OHJ[k][:, TILES:], io[:, 0:TILES], jf[:, bass.ds(n, 1)], io[:, bass.ds(t + 1, 1)],
                                ALU.is_equal, ALU.mult).then_inc(onehots, 1)
            for k in range(TOPK):
                onehot(0, k)
            with dve.Fori(1, NT) as t:
                for k in range(TOPK):
                    onehot(t, k)
            dve.wait_ge(inverted, TOPK * NT)
            st.then(v.tensor_copy(inv[:], bank[1][:, 0:2 * TILES]))
            v.scalar_tensor_tensor(ix[:], inv[:, TILES:], float(P), inv[:, 0:TILES], ALU.mult, ALU.add)
            st.then(v.tensor_scalar(fil[:], inv[:, TILES:], 0.0, io[:, P + 1:P + 2], ALU.is_equal, ALU.mult))
            st.then(v.tensor_tensor(ix[:], ix[:], fil[:], ALU.add))
            v.tensor_scalar(index[:], ix[:], float(-P), None, ALU.add).then_inc(tables, 1)

            def low(j, i):
                dve.wait_ge(xh_ready, j + 1)
                wait(dve, up_ready, 2 * (j - 1))
                v.tensor_tensor(XL[i][:].rearrange("p k s -> p (k s)"), bank[4][:, 0:E],
                                XH[i][:].bitcast(F32).rearrange("p k s -> p (k s)"),
                                ALU.subtract).then_inc(xl_ready, 1)

            def expert(j, x):
                i = x % 2
                up, ahead, down = stages(j)
                if up:
                    dve.wait_ge(sg_ready, j + 1)
                    dve.wait_ge(up_ready, 2 * (j + 1))
                    wait(dve, ht_psum, j - 1)
                    v.tensor_tensor(HD[i][:], SG[i][:], bank[2 * i + 1][:], ALU.mult).then_inc(hd_ready, 1)
                if ahead:
                    low(j + 1, 1 - i)
                if down:
                    o = 1 - i
                    dve.wait_ge(y_psum, j)
                    dve.wait_ge(pc_ready, j)
                    wait(dve, y_added, 16 * (j - 2))
                    v.tensor_scalar(YS[o][:], bank[6][:, 0:E], PC[(x - 1) % NX][:, 0:1], None, ALU.mult).then_inc(ys_ready, 1)
            low(0, 0)
            expert_tiles(dve, expert)

        @block.gpsimd
        def _(pool):
            q = nc.gpsimd

            def low(piece, i):
                pool.wait_ge(w_hi, piece + 1)
                at = bass.ds(piece * HID, HID)
                q.tensor_tensor(w12l[:].rearrange("p e k h -> p (e k h)")[:, at], wst[i][:],
                                w12h[:].bitcast(F32).rearrange("p e k h -> p (e k h)")[:, at],
                                ALU.subtract).then_inc(w_lo, 1)

            def stage1(b, x):
                if has(b, 0):
                    low(b, x % 2)
            gating(pool, stage1)
            pool.wait_ge(cols_ready, 1)

            def step(b, i):
                pb, o = b - 2, 1 - i
                if has(b, 0):
                    pool.wait_ge(in3[i], 16 * LOADS3 * ((b - i) // 2 + 1) if isinstance(b, int)
                                 else (b - i) * (8 * LOADS3) + 16 * LOADS3)
                    wait(pool, inter_ready, b - 1)
                    q.tensor_tensor(VW[i][:], AUG[i][:, 0],
                                    cols[:, 0, bass.ds(b * NH, NH)].unsqueeze(2).broadcast_to([P, NH, DV]),
                                    ALU.mult).then_inc(vw_ready, 1)
                if has(b, 2):
                    parts_ = [TOT[i][:, c * NH:(c + 1) * NH, 0:DH] for c in range(NC)]
                    pool.wait_ge(sc_ready, pb + 1)
                    for c in range(NC):
                        ins = q.tensor_tensor(parts_[c], parts_[c], sc[:, c * NH:(c + 1) * NH].unsqueeze(2)
                                              .broadcast_to([P, NH, DH]), ALU.mult).then_inc(mix_steps, 1)
                    for c in range(NC):
                        pool.wait_ge(mix_steps, 2 * NC * pb + c + 1)
                        if c == NC - 1:
                            pool.sem_inc(y_done, 1)
                        q.tensor_tensor(parts_[c], parts_[c], onwb[:], ALU.mult).then_inc(mix_steps, 1)
                    pool.wait_ge(inx[i], 8 * (pb - i) + 16)
                    for c in range(NC):
                        pool.wait_ge(mix_steps, 2 * NC * pb + NC + c + 1)
                        ins = q.tensor_tensor(X[i][:, c], X[i][:, c], parts_[c], ALU.add)
                    ins.then_inc(x2_ready, 1)
                if has(b, 1):
                    low(b - 1 + B, o)
            mixing(pool, step)

            def gather(j, x):
                wait(pool, xt_psum, j - NX + 1)
                wait(pool, pc_ready, j - NX + 1)
                pool.sem_inc(pool_carrier, 1)
                q.tensor_copy(IXG[x][:], index[:, bass.ds(j, 1)]).then_inc(ixg_ready, 1)
                pool.wait_ge(ixg_ready, j + 1)
                pool.sem_inc(pool_carrier, 1)
                q.indirect_dma_start(out=XG[x][:], out_offset=None, in_=table,
                                     in_offset=bass.IndirectOffsetOnAxis(ap=IXG[x][:, 0:1], axis=0)
                                     ).then_inc(xg_in[x], 16)

            def add(j, i):
                wait(pool, y_added, 16 * j)
                pool.sem_inc(pool_carrier, 1)
                q.tensor_copy(IXS[i][:], index[:, bass.ds(j, 1)]).then_inc(ixs_ready, 1)
                pool.wait_ge(ixs_ready, j + 1)
                pool.wait_ge(ys_ready, j + 1)
                pool.sem_inc(pool_carrier, 1)
                q.indirect_dma_start(out=out, out_offset=bass.IndirectOffsetOnAxis(ap=IXS[i][:, 0:1], axis=0),
                                     in_=YS[i][:], in_offset=None, compute_op=ALU.add).then_inc(y_added, 16)

            def expert(j, x):
                if not isinstance(j, int) or j + NX - 1 < TILES:
                    gather(j + NX - 1, (x - 1) % NX)
                if stages(j)[2]:
                    add(j - 1, 1 - x % 2)

            pool.wait_ge(tables, 1)
            pool.wait_ge(probs_out, 16)
            for i in range(2):
                pool.wait_ge(x_out[i], 16 * (B // 2))
                pool.wait_ge(row_out[i], 16 * (B // 2))
            pool.wait_ge(zero_out, 32)
            for x in range(NX - 1):
                gather(x, x)
            expert_tiles(pool, expert)
            pool.wait_ge(y_added, 16 * TILES)

        @block.tensor
        def _(pe):
            mm = nc.tensor.matmul
            pe.wait_ge(consts_in, 16 * N_CONST)
            pe.wait_ge(gc_ready, 1)

            def turn(b, i):
                pe.wait_ge(q_ready, b + 1)
                wait(pe, qT_ready, b - 1)
                for k in range(NK):
                    for c in range(NC):
                        ins = nc.tensor.transpose(bank[i][:, k * S + c * P:k * S + (c + 1) * P],
                                                  Q1[i][:, c, k * P:(k + 1) * P], id_f[:])
                ins.then_inc(qT_psum, 1)

            def gates(b, x):
                pe.wait_ge(qT_ready, b + 1)
                pe.wait_ge(ct1_in[x], 4 * (b - x) + 16)
                wait(pe, gates_ready, b - 1)
                i = x % 2
                o = bank[2 + i][0:2 * NH, 0:S]
                for k in range(NK):
                    mm(o, gq[:, k, :], QT1[i][:, k, :], start=(k == 0), stop=False)
                for k in range(NK):
                    ins = mm(o, gc[:, k, :], CT1[x][:, k, :], start=False, stop=(k == NK - 1))
                ins.then_inc(gates_psum, 1)

            def stage1(b, x):
                if has(b, 1):
                    turn(b - 1, 1 - x % 2)
                if has(b, 2):
                    gates(b - 2, (x - 2) % 4)
            gating(pe, stage1)

            pe.wait_ge(dcol_ready, 1)
            for k in range(4):
                ins = nc.tensor.transpose(bank[0][:, k * P:(k + 1) * P], dcol[:, k, :], id_f[:])
            ins.then_inc(cols_psum, 1)
            pe.wait_ge(cols_ready, 1)
            pe.wait_ge(marks_in, 64)

            def step(b, i):
                main, late, o = has(b, 0), has(b, 3), 1 - i

                def exponents(n):
                    c, hg = n // NG, n % NG
                    k = b * 2 * NG + n
                    wait(pe, d_ready, k - 1)
                    mm(bank[n % 2][:], LG[i][:, c * P:(c + 1) * P],
                       RM[i][:, hg * HG:(hg + 1) * HG, c * P:(c + 1) * P], start=True, stop=False)
                    mm(bank[n % 2][:], id_b[:], mask4[:], start=False, stop=True).then_inc(e_ready, 1)
                    wait(pe, c_ready, k - 1)
                    mm(bank[2 + n % 2][:], KT[i][:, hg, c * P:(c + 1) * P],
                       QBD[i][:, hg, :, c * P:(c + 1) * P], start=True, stop=True).then_inc(s_ready, 1)

                def values(n):
                    c, hg = n // NG, n % NG
                    pe.wait_ge(c_ready, b * 2 * NG + n + 1)
                    if n == 0:
                        wait(pe, o0_taken, b)
                    if n == NG:
                        wait(pe, o1_taken, b)
                    for j in range(HG):
                        h = hg * HG + j
                        ins = mm(bank[4 + c][:, h * DV:(h + 1) * DV], C[n % 2][:, j * P:(j + 1) * P],
                                 AUG[i][:, c, h, :], start=True, stop=True)
                    ins.then_inc(pv_group, 1)

                if main:
                    pe.wait_ge(in3[i], 16 * LOADS3 * ((b - i) // 2 + 1) if isinstance(b, int)
                               else (b - i) * (8 * LOADS3) + 16 * LOADS3)
                    exponents(0)
                    exponents(1)
                    pe.wait_ge(vw_ready, b + 1)
                    wait(pe, score_ready, b - 3)
                    wait(pe, kvb_ready, HG * b)
                    for n in range(NG):
                        ins = mm(bank[6][:, n * HG * DV:(n + 1) * HG * DV], KN[i][:, n * P:(n + 1) * P],
                                 VW[i][:, n * HG:(n + 1) * HG, :], start=True, stop=True)
                    ins.then_inc(kv_psum, 1)
                    values(0)
                    exponents(2)
                if late:
                    pe.wait_ge(x2n_ready, b - 2)
                    pe.wait_ge(o1_taken, min(b, B) if isinstance(b, int) else b)
                    for n in range(NC * NK):
                        ins = nc.tensor.transpose(bank[7][:, n * P:(n + 1) * P],
                                                  X2N[o][:, n // NK, n % NK * P:(n % NK + 1) * P], id_f[:])
                    ins.then_inc(x2t_psum, 1)
                if main:
                    values(1)
                    exponents(3)
                    values(2)
                if late:
                    pe.wait_ge(x2t_ready, b - 2)
                    wait(pe, score_ready, b - 3)
                    if main:
                        pe.wait_ge(kvb_ready, HG * (b + 1))
                    for c in range(NC):
                        at = NH * DV + c * NE
                        for k in range(NK):
                            ins = mm(bank[6][:, at:at + NE], X2T[:, c * NK + k, :], gate_w[:, k, :],
                                     start=(k == 0), stop=(k == NK - 1))
                    ins.then_inc(score_psum, 1)
                if main:
                    values(3)
                    pe.wait_ge(kvb_ready, HG * (b + 1))
                    wait(pe, o1_taken, b)
                    wait(pe, x2t_ready, b - 2)
                    for n in range(NG):
                        ins = mm(bank[7][:, n * HG * DV:(n + 1) * HG * DV], QTB[i][:, n, :],
                                 KVB[i][:, n].rearrange("p j d -> p (j d)"), start=True, stop=True)
                    ins.then_inc(inter_ready, 1)
            mixing(pe, step)

            pe.wait_ge(r_ones, 1)
            mm(bank[0][:, 0:SCN], tri[:, 0, :], abf[:], start=True, stop=True)
            mm(bank[0][:, SCN:2 * SCN], tri[:, 1, :], abf[:], start=True, stop=True).then_inc(r_counts, 1)

            def invert(n, k, start=False, stop=False):
                pe.wait_ge(onehots, n + 1)
                mm(bank[1][:, 0:2 * TILES], OHP[k][:], OHJ[k][:], start=start, stop=stop).then_inc(inverted, 1)
            for k in range(TOPK):
                invert(k, k, start=(k == 0))
            with pe.Fori(1, NT - 1) as t:
                for k in range(TOPK):
                    invert(t * TOPK + k, k)
            for k in range(TOPK):
                invert((NT - 1) * TOPK + k, k, stop=(k == TOPK - 1))

            def rows(j, x):
                pe.wait_ge(xg_in[x], (16 // NX) * (j - x) + 16)
                wait(pe, xl_ready, j)
                for k in range(NK):
                    ins = nc.tensor.transpose(bank[4][:, k * P:(k + 1) * P], XG[x][:, k * P:(k + 1) * P], id_f[:])
                ins.then_inc(xt_psum, 1)

            def expert(j, x):
                i, o = x % 2, 1 - x % 2
                up, ahead, down = stages(j)

                def half_up(half):
                    acc = bank[2 * i + half][:]
                    for k in range(NK):
                        wh = w12h[:, bass.ds(e, 1), k, half * HID:(half + 1) * HID].rearrange("p a h -> p (a h)")
                        wl = w12l[:, bass.ds(e, 1), k, half * HID:(half + 1) * HID].rearrange("p a h -> p (a h)")
                        mm(acc, XH[i][:, k, :], wl, start=(k == 0), stop=False)
                        mm(acc, XL[i][:, k, :], wh, start=False, stop=False)
                        ins = mm(acc, XH[i][:, k, :], wh, start=False, stop=(k == NK - 1))
                    ins.then_inc(up_ready, 1)

                if up:
                    e = pe.value_load(etab[0:1, bass.ds(j, 1)], min_val=0, max_val=NE - 1)
                    pe.wait_ge(xl_ready, j + 1)
                    wait(pe, hd_ready, j - 1)
                    half_up(0)
                if down:
                    pe.wait_ge(hd_ready, j)
                    wait(pe, ht_ready, j - 1)
                    for k in range(KH):
                        ins = nc.tensor.transpose(bank[5][:, k * P:(k + 1) * P], HD[o][:, k * P:(k + 1) * P], id_f[:])
                    ins.then_inc(ht_psum, 1)
                if up:
                    half_up(1)
                if ahead:
                    rows(j + 1, (x + 1) % NX)
                if down:
                    ed = pe.value_load(etab[0:1, bass.ds(j - 1, 1)], min_val=0, max_val=NE - 1)
                    pe.wait_ge(ht_ready, j)
                    wait(pe, ys_ready, j - 1)
                    for k in range(KH):
                        ins = mm(bank[6][:, 0:E], HT[o][:, k, :],
                                 w3[:, bass.ds(ed, 1), k, :].rearrange("p a d -> p (a d)"),
                                 start=(k == 0), stop=(k == KH - 1))
                    ins.then_inc(y_psum, 1)

            pe.wait_ge(tables, 1)
            pe.wait_ge(w3_in, 16 * NE)
            rows(0, 0)
            expert_tiles(pe, expert)


_OUT = (ROWS, E)


def kernel(x, ctx_1024, L0_xattn_igate_kernel, L0_xattn_igate_bias, L0_xattn_fgate_kernel,
           L0_xattn_fgate_bias, L0_xattn_outnorm_weight, L0_ffn_w12, L0_ffn_w3, L0_ffn_gate_w):
    import ml_dtypes
    import concourse.bacc as bacc
    from concourse.bass_utils import run_bass_kernel_spmd as run

    bf = ml_dtypes.bfloat16
    a = {k: np.asarray(v) for k, v in dict(
        x=x, ctx=ctx_1024, ik=L0_xattn_igate_kernel, ib=L0_xattn_igate_bias, fk=L0_xattn_fgate_kernel,
        fb=L0_xattn_fgate_bias, onw=L0_xattn_outnorm_weight, w12=L0_ffn_w12, w3=L0_ffn_w3,
        gate=L0_ffn_gate_w).items()}
    ctx2 = a["ctx"].reshape(N, E)
    gk = np.concatenate([a["ik"], a["fk"]], axis=1).reshape(3, NK, P, 2 * NH).transpose(0, 2, 1, 3).reshape(3, P, -1)
    p, q = np.arange(P)[:, None], np.arange(P)[None, :]
    marks = np.ones((PARTS * (NH + 1), NH * S), np.float32)
    marks[PARTS:] = np.tile(np.repeat(np.eye(NH), S, axis=1), (PARTS, 1))
    ins = {
        "x": a["x"].reshape(N, E),
        "ctx": ctx2,
        "ctxv": np.concatenate([ctx2.reshape(N, NH, DH), np.ones((N, NH, 1), np.float32)], axis=2).reshape(N, NH * DV),
        "ctxT": ctx2.T,
        "gkq": gk[0], "gkk": gk[1], "gkv": gk[2],
        "ibias": np.tile(a["ib"], B)[:, None],
        "fbias": np.tile(a["fb"], B)[:, None],
        "onw": np.broadcast_to(a["onw"].reshape(1, E), (P, E)),
        "w12T": a["w12"].transpose(2, 0, 1).reshape(NK, P, NE, 2 * HID).transpose(1, 2, 0, 3).reshape(P, -1),
        "w3T": a["w3"].transpose(2, 0, 1).reshape(KH, P, NE, E).transpose(1, 2, 0, 3).reshape(P, -1),
        "gateT": a["gate"].T.reshape(NK, P, NE).transpose(1, 0, 2).reshape(P, -1),
        "ident": np.eye(P, dtype=np.float32),
        "identb": np.eye(P).astype(bf),
        "maskT": np.tile(np.where(p > q, MASKED, 0.0), (1, HG)).astype(bf),
        "trib": np.concatenate([p < q, np.ones((P, P))], axis=1).astype(bf),
        "marks": marks.astype(bf),
        "iota": np.concatenate([np.broadcast_to(q, (P, P)), p, N + P + p], axis=1).astype(np.float32),
    }
    nc = bacc.Bacc("TRN2", target_bir_lowering=False, num_devices=1)
    arrays, args = {}, []
    for name, v in ins.items():
        arrays["in_" + name] = np.ascontiguousarray(v)
        args.append(nc.dram_tensor("in_" + name, v.shape, mybir.dt.from_np(v.dtype), kind="ExternalInput").ap())
    args.append(nc.dram_tensor("out_rows", _OUT, F32, kind="ExternalOutput").ap())
    build(nc, *args)
    r = run(nc, [arrays], core_ids=[0])
    return r.results[0]["out_rows"][0:N].reshape(B, S, E)
```

```python
from contextlib import ExitStack

import numpy as np

import concourse.bass as bass
from concourse import mybir

ALU = mybir.AluOpType
ACT = mybir.ActivationFunctionType
AX = mybir.AxisListType
F32 = mybir.dt.float32
F32R = mybir.dt.float32r
BF16 = mybir.dt.bfloat16
I32 = mybir.dt.int32
U32 = mybir.dt.uint32

P = 128
B, S, E = 16, 256, 256
NH, DH = 8, 32
NE, HID = 8, 512
TOPK = 2
NC = S // P
NK = E // P
HG = P // DH
NG = NH // HG
DV = DH + 1
N = B * S
NT = N // P
TILES = (N * TOPK + NE * (P - 1)) // P
ROWS = N + P
ROW = E + NE
KH = HID // P
NX = 4
NI = 4
KS = float(DH) ** -0.5
LN_EPS, HEAD_EPS, NORM_EPS = 1e-5, 1e-6, 1e-6
PARTS = 3
MASKED = -1e30


def wait(eng, sem, value):
    if isinstance(value, int) and value <= 0:
        return
    eng.wait_ge(sem, value)


class Steps:

    def __init__(self, eng, sem, base):
        self.eng, self.sem, self.base, self.n = eng, sem, base, 0

    def then(self, ins):
        ins.then_inc(self.sem, 1)
        self.n += 1
        self.eng.wait_ge(self.sem, self.base + self.n)


def build(nc, x, ctx, ctxv, ctxT, gkq, gkk, gkv, ibias, fbias, onw, w12T, w3T, gateT, ident, identb,
          maskT, trib, marks, iota, nums, out):
    qT_dram = nc.dram_tensor("qT_scratch", (B, P, NG, S), F32).ap()
    gate_dram = nc.dram_tensor("gate_scratch", (B, 2 * NH, S), F32).ap()
    negM_dram = nc.dram_tensor("negM_scratch", (PARTS, B * NH, S), BF16).ap()
    g_dram = nc.dram_tensor("g_scratch", (B, PARTS, NH, S), BF16).ap()
    table = nc.dram_tensor("token_table", (ROWS, ROW), F32).ap()

    x_t = x.rearrange("(b c p) e -> b p c e", c=NC, p=P)
    ctx_t = ctx.rearrange("(b c p) e -> b p c e", c=NC, p=P)
    ctxv_t = ctxv.rearrange("(b c p) e -> b p c e", c=NC, p=P)
    ctxT_t = ctxT.rearrange("(k p) (b s) -> b p k s", p=P, s=S)
    out_t = out[0:N, :].rearrange("(b c p) e -> b p c e", c=NC, p=P)
    table_t = table[0:N, 0:E].rearrange("(b c p) e -> b p c e", c=NC, p=P)

    with ExitStack() as stack:
        def sb(name, shape, dt=F32, on=None):
            return (on or stack).enter_context(nc.sbuf_tensor(name, shape, dt))

        def sem(name):
            return stack.enter_context(nc.semaphore(name))

        bank = [stack.enter_context(nc.psum_tensor(f"bank{i}", [P, 512], F32)) for i in range(8)]

        w12h = sb("w12h", [P, NE, NK, 2 * HID], F32R)
        w12l = sb("w12l", [P, NE, NK, 2 * HID], F32R)
        id_f = sb("id_f", [P, P])
        id_b = sb("id_b", [P, P], BF16)
        tri = sb("tri", [P, 2, P], BF16)
        io = sb("io", [P, P + 1])
        numbers = sb("numbers", [P, 2 * TOPK * NT])
        gate_w = sb("gate_w", [P, NK, NE])
        scores = sb("scores", [P, NT, NE])
        etab = sb("etab", [P, TILES], I32)
        index = sb("index", [P, TILES], U32)

        early = ExitStack()
        cols = sb("cols", [P, 4, B * NH], on=early)
        eps = sb("eps", [P, 2], on=early)
        onwb = sb("onwb", [P, NH, DH], on=early)
        mask4 = sb("mask4", [P, HG * P], BF16, on=early)
        wst = [sb(f"wst{i}", [P, HID], on=early) for i in range(2)]
        KT = [sb(f"kt{i}", [P, NG, S], on=early) for i in range(2)]
        KVB = [sb(f"kvb{i}", [P, NG, HG, DV], on=early) for i in range(2)]
        RM = [sb(f"rm{i}", [PARTS * (NH + 1), NH, S], BF16, on=early) for i in range(2)]
        LG = [sb(f"lg{i}", [PARTS * (NH + 1), S], BF16, on=early) for i in range(2)]
        QBD = [sb(f"qbd{i}", [P, NG, HG, S], on=early) for i in range(2)]

        a = ExitStack()
        gq, gk, gv, gc = (sb(n, [P, NK, 2 * NH], on=a) for n in ("gq", "gk", "gv", "gc"))
        ib, fb = (sb(n, [P, 1], on=a) for n in ("ib", "fb"))
        Q1 = [sb(f"q1_{i}", [P, NC, E], on=a) for i in range(2)]
        QT1 = [sb(f"qt1_{i}", [P, NK, S], on=a) for i in range(2)]
        GS1 = [sb(f"gs1_{i}", [2 * NH, S], on=a) for i in range(2)]
        st1 = [sb(f"st1_{i}", [P, NC, 6], on=a) for i in range(4)]
        mv1 = [sb(f"mv1_{i}", [P, NC, 2], on=a) for i in range(4)]
        lnv1 = [sb(f"lnv1_{i}", [P, NC], on=a) for i in range(4)]
        rs1 = [sb(f"rs1_{i}", [P, NC], on=a) for i in range(4)]
        parts = sb("parts", [P, 2, PARTS, S], BF16, on=a)
        rest = sb("rest", [P, 2, PARTS - 1, S], on=a)
        zeros = sb("zeros", [P, S], on=a)
        zrow = sb("zrow", [P, ROW], on=a)
        a1 = ExitStack()
        X1 = [sb(f"x1_{i}", [P, NC, E], on=a1) for i in range(4)]
        CT1 = [sb(f"ct1_{i}", [P, NK, S], on=a1) for i in range(4)]
        a1.close()
        gi, gf, fa, fm, fe, fl, lsg, cs, g, M, negM, mx = (
            sb(n, [P, S], on=a) for n in ("gi", "gf", "fa", "fm", "fe", "fl", "lsg", "cs", "g_", "M_",
                                          "negM", "mx"))
        dcol = sb("dcol", [P, 4, P], on=a)
        a.close()

        m = ExitStack()
        QTB = [sb(f"qtb{i}", [P, NG, P], on=m) for i in range(2)]
        KN = [sb(f"kn{i}", [P, E], on=m) for i in range(2)]
        AUG = [sb(f"aug{i}", [P, NC, NH, DV], on=m) for i in range(2)]
        VW = [sb(f"vw{i}", [P, NH, DV], on=m) for i in range(2)]
        D = [sb(f"d{i}", [P, HG * P], on=m) for i in range(2)]
        C = [sb(f"c{i}", [P, HG * P], on=m) for i in range(2)]
        X = [sb(f"x3_{i}", [P, NC, NH, DH], on=m) for i in range(2)]
        TOT = [sb(f"tot{i}", [P, NC * NH, DV], on=m) for i in range(2)]
        X2N = [sb(f"x2n{i}", [P, NC, E], on=m) for i in range(2)]
        X2T = sb("x2t", [P, NC * NK, P], on=m)
        wabs, wmax, wden, rec, mu, var, z, z2, lnz, zp, sc = (
            sb(n, [P, NC * NH], on=m)
            for n in ("wabs", "wmax", "wden", "rec", "mu", "var", "z_", "z2_", "lnz", "zp", "sc"))
        st3 = sb("st3", [P, NC, 6], on=m)
        mv3 = sb("mv3", [P, NC, 2], on=m)
        lnv3 = sb("lnv3", [P, NC], on=m)
        rs3 = sb("rs3", [P, NC], on=m)
        m.close()
        early.close()

        f = ExitStack()
        w3 = sb("w3", [P, NE, KH, E], on=f)
        r = ExitStack()
        SCN = NT * NE

        def rt(name, w, dt=F32):
            return sb(name, [P, w], dt, on=r)

        m1, m2, first, ex, den2, p1, p2, zer = (
            rt(n, NT) for n in ("m1", "m2", "first", "ex", "den2", "p1", "p2", "zer"))
        ta, tb, oh1, oh2, s2, pw, cum, slotS = (
            rt(n, SCN) for n in ("ta", "tb", "oh1", "oh2", "s2", "pw", "cum", "slotS"))
        abf = rt("abf", SCN, BF16)
        slot, jf, pf = (rt(n, TOPK * NT) for n in ("slot", "jf", "pf"))
        sloti, sj, sp_ = (rt(n, TOPK * NT, I32) for n in ("sloti", "sj", "sp_"))
        nef, base = rt("nef", NE), rt("base", NE + 1)
        nei, neb = rt("nei", NE, I32), rt("neb", NE, I32)
        OHP = [rt(f"ohp{i}", NI * P, BF16) for i in range(4)]
        OHJ = [rt(f"ohj{i}", NI * TILES) for i in range(4)]
        OHN = [rt(f"ohn{i}", NI * 2 * TILES, BF16) for i in range(4)]
        fil, count = rt("fil", TILES), rt("count", TILES)
        later = rt("later", TILES * (NE - 1))
        r.close()
        XG = [sb(f"xg{i}", [P, ROW], on=f) for i in range(NX)]
        XH = [sb(f"xh{i}", [P, NK, P], F32R, on=f) for i in range(2)]
        XL = [sb(f"xl{i}", [P, NK, P], F32R, on=f) for i in range(2)]
        SG = [sb(f"sg{i}", [P, HID], on=f) for i in range(2)]
        HD = [sb(f"hd{i}", [P, HID], on=f) for i in range(2)]
        HTH = [sb(f"hth{i}", [P, KH, P], F32R, on=f) for i in range(2)]
        HTL = [sb(f"htl{i}", [P, KH, P], F32R, on=f) for i in range(2)]
        W3H = [sb(f"w3h{i}", [P, KH * E], F32R, on=f) for i in range(2)]
        W3L = [sb(f"w3l{i}", [P, KH * E], F32R, on=f) for i in range(2)]
        YS = [sb(f"ys{i}", [P, E], on=f) for i in range(2)]
        PC = [sb(f"pc{i}", [P, 1], on=f) for i in range(NX)]
        IXG = [sb(f"ixg{i}", [P, 1], U32, on=f) for i in range(NX)]
        IXS = [sb(f"ixs{i}", [P, 1], U32, on=f) for i in range(2)]
        f.close()

        def sems(*names):
            return tuple(sem(n) for n in names)

        def two(name):
            return [sem(f"{name}_{i}") for i in range(2)]

        consts_in, zero_rows, zero_out = sems("consts_in", "zero_rows", "zero_out")
        dve_carrier, pool_carrier = sems("dve_carrier", "pool_carrier")
        qT_out, gate_out = two("qT_out"), two("gate_out")
        x1_in, ct1_in = ([sem(f"{n}_{i}") for i in range(4)] for n in ("x1_in", "ct1_in"))
        ln1_steps, ln1_log, ln1_rstd, q_ready, eps_set = sems(
            "ln1_steps", "ln1_log", "ln1_rstd", "q_ready", "eps_set")
        qT_psum, qT_ready, gates_psum, gates_ready, gc_ready = sems(
            "qT_psum", "qT_ready", "gates_psum", "gates_ready", "gc_ready")
        pair_in, pair_dve, pair_act, m_parts, g_parts, g_there, g_rest, parts_out = sems(
            "pair_in", "pair_dve", "pair_act", "m_parts", "g_parts", "g_there", "g_rest", "parts_out")
        abs_ready, log_ready, g_ready, dcol_ready, cols_psum, cols_ready = sems(
            "abs_ready", "log_ready", "g_ready", "dcol_ready", "cols_psum", "cols_ready")
        wst_in = two("wst_in")
        pieces2_in = [sem(f"pieces2_in_{n}") for n in range(B // 2 - 2)]
        w_hi, w_lo = sems("w_hi", "w_lo")
        in3, inv3, inx, x_out, row_out = two("in3"), two("inv3"), two("inx"), two("x_out"), two("row_out")
        zeroed, late_consts, y_done, tail_steps = sems("zeroed", "late_consts", "y_done", "tail_steps")
        e_ready, d_ready, s_ready, c_ready = sems("e_ready", "d_ready", "s_ready", "c_ready")
        vw_ready, kv_psum, kvb_ready, pv_group, inter_ready = sems(
            "vw_ready", "kv_psum", "kvb_ready", "pv_group", "inter_ready")
        o0_taken, o1_taken, post_steps, cen_ready, sq_ready = sems(
            "o0_taken", "o1_taken", "post_steps", "cen_ready", "sq_ready")
        z_ready, z_log, zpow_ready, sc_ready, mix_steps, x2_ready = sems(
            "z_ready", "z_log", "zpow_ready", "sc_ready", "mix_steps", "x2_ready")
        late_steps, var3_log, rstd3, x2n_ready = sems("late_steps", "var3_log", "rstd3", "x2n_ready")
        x2t_psum, x2t_ready, score_psum, score_ready = sems(
            "x2t_psum", "x2t_ready", "score_psum", "score_ready")
        w3_in, r_steps, r_diff, r_exp, r_ones, r_counts, probs_ready, probs_out = sems(
            "w3_in", "r_steps", "r_diff", "r_exp", "r_ones", "r_counts", "probs_ready", "probs_out")
        hots_made, hots_ready, inverted, tables = sems("hots_made", "hots_ready", "inverted", "tables")
        ixg_ready, ixs_ready, y_added = sems("ixg_ready", "ixs_ready", "y_added")
        xg_in = [sem(f"xg_in_{i}") for i in range(NX)]
        xt_psum, xh_ready, xl_ready, up_ready, sg_ready, hd_ready = sems(
            "xt_psum", "xh_ready", "xl_ready", "up_ready", "sg_ready", "hd_ready")
        ht_psum, hth_ready, htl_ready, y_psum, ys_ready, pc_ready = sems(
            "ht_psum", "hth_ready", "htl_ready", "y_psum", "ys_ready", "pc_ready")
        w3h_ready, w3l_ready = sems("w3h_ready", "w3l_ready")

        def gating(eng, step, peeled=4):
            for b in range(peeled):
                step(b, b % 4)
            with eng.Fori(peeled // 4, B // 4) as it:
                for x in range(4):
                    step(it * 4 + x, x)
            for b in range(B, B + 2):
                step(b, b % 4)

        def mixing(eng, step):
            for b in range(4):
                step(b, b % 2)
            with eng.Fori(2, B // 2) as it:
                step(it * 2, 0)
                step(it * 2 + 1, 1)
            for b in range(B, B + 3):
                step(b, b % 2)

        def has(b, back):
            return not isinstance(b, int) or 0 <= b - back < B

        def inversion(eng, step):
            steps = TOPK * NT // NI
            for m in range(4):
                step(m, m)
            with eng.Fori(1, steps // 4 - 1) as it:
                for i in range(4):
                    step(it * 4 + i, i)
            for m in range(steps - 4, steps):
                step(m, m % 4)

        def expert_tiles(eng, step):
            for j in range(NX):
                step(j, j)
            with eng.Fori(1, TILES // NX) as it:
                for x in range(NX):
                    step(it * NX + x, x)
            for x in range(NX):
                step(TILES // NX * NX + x, x)

        def stages(j):
            if not isinstance(j, int):
                return True, True, True
            return j < TILES, j + 1 < TILES, j >= 1

        def flat(t):
            return t[:].rearrange("p k s -> p (k s)")

        N_CONST, N_LATE = 4, 13
        PIECES0, PIECES2 = (0, 2), tuple(range(4, B, 2))
        W0 = len(PIECES0)
        EARLY2 = 2
        W1 = W0 + B
        W2 = W1 + len(PIECES2)
        BUF2 = [flat(t) for t in (Q1[0], Q1[1], QT1[0], QT1[1])] + [t[:] for t in wst]
        IN0, IN1 = 16 * W0 // 2, 16 * (W0 + B // 2) // 2
        K1 = 2 * NC
        LOADS3 = 1 + HG + 2
        LOADSV = 3

        def load2(eng, n):
            at = PIECES2[n] * HID
            eng.dma_start(BUF2[n], w12T[:, at:at + HID]).then_inc(pieces2_in[n], 16)

        def loaded(b, i, n):
            return 16 * n * ((b - i) // 2 + 1) if isinstance(b, int) else (b - i) * (8 * n) + 16 * n

        def three_parts(eng, ops, src, k, counter):
            for q in range(PARTS):
                ops.tensor_copy(parts[:, k, q, :], src[:]).then_inc(counter, 1)
                if q + 1 < PARTS:
                    eng.wait_ge(counter, 2 * q + 1)
                    ops.tensor_tensor(rest[:, k, q, :], src[:], parts[:, k, q, :], ALU.subtract).then_inc(counter, 1)
                    eng.wait_ge(counter, 2 * q + 2)
                    src = rest[:, k, q, :]

        block = stack.enter_context(nc.Block())

        @block.sync
        def _(sp):
            for b in range(2):
                sp.dma_start(X1[b][:], x_t[b]).then_inc(x1_in[b], 16)
            sp.dma_start(id_f[:], ident).then_inc(consts_in, 16)
            for dst, src in ((gq, gkq), (gk, gkk), (gv, gkv)):
                sp.dma_start(dst[:], src.rearrange("p (k g) -> p k g", k=NK)).then_inc(consts_in, 16)

            def later_constants():
                for dst, src in ((ib, ibias), (fb, fbias), (id_b, identb), (mask4, maskT), (io, iota), (numbers, nums)):
                    sp.dma_start(dst[:], src).then_inc(late_consts, 16)
                sp.dma_start(gate_w[:], gateT.rearrange("p (k g) -> p k g", k=NK)).then_inc(late_consts, 16)
                sp.dma_start(tri[:], trib.rearrange("p (a q) -> p a q", a=2)).then_inc(late_consts, 16)
                sp.dma_start(onwb[:], onw.rearrange("p (h d) -> p h d", h=NH)).then_inc(late_consts, 16)
                for i in range(2):
                    sp.dma_start(LG[i][0:PARTS, :], marks[0:PARTS, 0:S]).then_inc(late_consts, 16)
                    sp.dma_start(RM[i][PARTS:PARTS * (NH + 1), :, :],
                                 marks[PARTS:PARTS * (NH + 1), :].rearrange("q (h s) -> q h s", h=NH)
                                 ).then_inc(late_consts, 16)

                sp.wait_ge(zero_rows, 1)
                sp.dma_start(table[N:ROWS, :], zrow[:]).then_inc(zero_out, 16)
                sp.dma_start(out[N:ROWS, :], zrow[:, 0:E]).then_inc(zero_out, 16)

            def stage1(b, x):
                old, o = b - 5, 1 - x % 2
                if has(b, 0) and (not isinstance(b, int) or b >= 2):
                    wait(sp, q_ready, b - 3)
                    sp.dma_start(X1[x][:], x_t[b]).then_inc(x1_in[x], 16)
                if has(b, 5):
                    sp.wait_ge(qT_ready, old + 1)
                    sp.dma_start(qT_dram[old], QT1[o][:]).then_inc(qT_out[o], 16)
                if has(b, 1):
                    y = (x + 3) % 4
                    wait(sp, gates_psum, b - 4)
                    sp.dma_start(CT1[y][:], ctxT_t[b - 1]).then_inc(ct1_in[y], 16)
                if isinstance(b, int) and b == 3:
                    later_constants()
                if has(b, 5):
                    sp.wait_ge(gates_ready, old + 1)
                    sp.dma_start(gate_dram[old], GS1[o][:]).then_inc(gate_out[o], 16)
            gating(sp, stage1, peeled=8)
            for b in range(B + 2, B + 5):
                stage1(b, b % 4)

            for i in range(2):
                sp.wait_ge(gate_out[i], 16 * (B // 2))
            for k, dst in enumerate((gi, gf)):
                sp.dma_start(dst[:], gate_dram[:, k * NH:(k + 1) * NH, :]).then_inc(pair_in, 16)

            def load_scores(b, i):
                sp.dma_start(KT[i][:], ctxT_t[b]).then_inc(in3[i], 16)
                for j in range(HG):
                    sp.dma_start(QBD[i][j * DH:(j + 1) * DH, :, j, :],
                                 qT_dram[b, j * DH:(j + 1) * DH]).then_inc(in3[i], 16)

            for i in range(2):
                sp.wait_ge(qT_out[i], 16 * (B // 2))
            sp.wait_ge(zeroed, 1)
            load_scores(0, 0)
            sp.wait_ge(gates_psum, B)
            sp.wait_ge(w_lo, W1)
            for n in range(EARLY2, len(PIECES2)):
                load2(sp, n)
            for q in range(PARTS):
                sp.wait_ge(g_parts, q + 1)
                sp.dma_start(g_dram[:, q], parts[:, 1, q, :]).then_inc(parts_out, 16)
            sp.wait_ge(m_parts, 2 * PARTS - 1)
            sp.dma_start(negM_dram.rearrange("a q s -> q a s"), parts[:, 0]).then_inc(parts_out, 16)
            sp.wait_ge(parts_out, 16 * (1 + PARTS))
            sp.wait_ge(zero_out, 32)
            sp.wait_ge(cols_ready, 1)

            def store(b, i):
                sp.wait_ge(x2n_ready, b + 1)
                sp.dma_start(out_t[b], X[i][:].rearrange("p c h d -> p c (h d)")).then_inc(x_out[i], 16)
                sp.dma_start(table_t[b], X2N[i][:]).then_inc(row_out[i], 16)

            def step(b, i):
                o = 1 - i
                if has(b, 0):
                    wait(sp, s_ready, 2 * NG * (b - 1))
                    sp.dma_start(LG[i][PARTS:, :], g_dram[b].rearrange("q h s -> (q h) s")).then_inc(in3[i], 16)
                    sp.dma_start(RM[i][0:PARTS, :, :],
                                 negM_dram[:, bass.ds(b * NH, NH), :]).then_inc(in3[i], 16)
                    if not isinstance(b, int) or b >= 1:
                        load_scores(b, i)
                if has(b, 2):
                    wait(sp, x_out[i], 8 * (b - 2 - i))
                    sp.dma_start(X[i][:].rearrange("p c h d -> p c (h d)"), x_t[b - 2]).then_inc(inx[i], 16)
                if has(b, 0):
                    wait(sp, inter_ready, b - 1)
                    if isinstance(b, int) and b == 0:
                        sp.wait_ge(w_lo, W2 - len(wst))
                    sp.dma_start(AUG[i][:].rearrange("p c h d -> p c (h d)"), ctxv_t[b]).then_inc(inv3[i], 16)
                    sp.dma_start(KN[i][:], ctx_t[b, :, 0, :]).then_inc(inv3[i], 16)
                    sp.dma_start(QTB[i][:], qT_dram[b, :, :, P:S]).then_inc(inv3[i], 16)
                if has(b, 3):
                    store(b - 3, o)
            mixing(sp, step)

            for i in range(2):
                sp.wait_ge(x_out[i], 16 * (B // 2))
                sp.wait_ge(row_out[i], 16 * (B // 2))
            sp.wait_ge(score_ready, B)
            sp.wait_ge(w_lo, W2 + B)
            for e in range(NE):
                sp.dma_start(w3[:, e], w3T[:, e * KH * E:(e + 1) * KH * E].rearrange(
                    "p (k d) -> p k d", k=KH)).then_inc(w3_in, 16)
            sp.wait_ge(probs_ready, 1)
            sp.dma_start(table[0:N, E:ROW].rearrange("(t p) e -> p t e", p=P),
                         pw[:].rearrange("p (t e) -> p t e", e=NE)).then_inc(probs_out, 16)
            sp.wait_ge(w3_in, 16 * NE)
            sp.wait_ge(probs_out, 16)

        @block.scalar
        def _(act):
            def power(out_, log_, in_, column, counter, n, ready):
                nc.scalar.activation(log_, in_, ACT.Ln, bias=eps[:, column:column + 1]).then_inc(counter, 1)
                act.wait_ge(counter, n)
                nc.scalar.activation(out_, log_, ACT.Exp, scale=-0.5).then_inc(ready, 1)

            def high(piece, src, count, arrived, steps=1):
                act.wait_ge(arrived, count)
                nc.scalar.copy(w12h[:].rearrange("p e k h -> p (e k h)")[:, bass.ds(piece * HID, HID)],
                               src).then_inc(w_hi, steps)

            def stage1(b, x):
                i, o = x % 2, 1 - x % 2
                if has(b, 0):
                    act.wait_ge(ln1_steps, K1 * (b + 1))
                    power(rs1[x][:], lnv1[x][:], mv1[x][:, :, 1], 0, ln1_log, b + 1, ln1_rstd)
                if has(b, 1):
                    a_ = b - 1
                    act.wait_ge(qT_psum, a_ + 1)
                    wait(act, gates_psum, a_ - 1)
                    wait(act, qT_out[o], 8 * (a_ - o))
                    nc.scalar.copy(QT1[o][:].rearrange("p k s -> p (k s)"), bank[o][:]).then_inc(qT_ready, 1)
                if has(b, 2):
                    a_ = b - 2
                    act.wait_ge(gates_psum, a_ + 1)
                    wait(act, gate_out[i], 8 * (a_ - i))
                    nc.scalar.copy(GS1[i][:], bank[2 + i][0:2 * NH, 0:S]).then_inc(gates_ready, 1)
                if x % 2 and has(b, 2):
                    old = (x - 2) % 4
                    high(b - 2, wst[old // 2][:], IN0 + 4 * (b - 2 - old) + 16, wst_in[old // 2], steps=2)
            nc.scalar.preload_act_table_set("natural_log_exp_and_others")
            for n, piece in enumerate(PIECES0):
                high(piece, wst[n][:], 16, wst_in[n])
            act.wait_ge(eps_set, 1)
            gating(act, stage1)

            def pieces2(lo, hi):
                for n in range(lo, hi):
                    high(PIECES2[n], BUF2[n], 16, pieces2_in[n])

            act.wait_ge(qT_psum, B)
            for n in range(EARLY2):
                load2(act, n)
            pieces2(0, EARLY2)
            act.wait_ge(pair_in, 32)
            nc.scalar.activation(fa[:], gf[:], ACT.Abs, bias=fb[:, 0:1]).then_inc(abs_ready, 1)
            act.wait_ge(abs_ready, 1)
            nc.scalar.activation(fe[:], fa[:], ACT.Exp, scale=-1.0).then_inc(pair_act, 1)
            act.wait_ge(pair_act, 1)
            nc.scalar.activation(fl[:], fe[:], ACT.Ln, bias=1.0).then_inc(log_ready, 1)
            for q in range(PARTS):
                act.wait_ge(g_rest, q + 1)
                src = g[:] if q == 0 else rest[:, 1, q - 1, :]
                nc.scalar.copy(parts[:, 1, q, :], src).then_inc(g_parts, 1)
            act.wait_ge(g_ready, 1)
            nc.scalar.activation(dcol[:, 0, :], g[:, 0:P], ACT.Exp, bias=negM[:, P - 1:P])
            nc.scalar.activation(dcol[:, 1, :], negM[:, P:S], ACT.Exp, bias=M[:, P - 1:P])
            nc.scalar.activation(dcol[:, 2:4, :].rearrange("p a s -> p (a s)"), mx[:], ACT.Exp,
                                 scale=-1.0).then_inc(dcol_ready, 1)
            pieces2(EARLY2, len(PIECES2))

            def step(b, i):
                o = 1 - i
                if has(b, 1):
                    act.wait_ge(pv_group, 2 * NG * (b - 1) + NG)
                    wait(act, x2_ready, b - 2)
                    nc.scalar.copy(TOT[o][:, 0:NH, :].rearrange("p h d -> p (h d)"),
                                   bank[4][:, 0:NH * DV]).then_inc(o0_taken, 1)

                def weights(n):
                    if has(b, 0):
                        k = b * 2 * NG + n
                        act.wait_ge(e_ready, k + 1)
                        wait(act, c_ready, k - 1)
                        nc.scalar.activation(D[n % 2][:], bank[n % 2][:], ACT.Exp).then_inc(d_ready, 1)

                weights(0)
                weights(1)
                if has(b, 0):
                    act.wait_ge(kv_psum, b + 1)
                    wait(act, inter_ready, b - 1)
                    for j in range(HG):
                        lo, hi = j * DH, (j + 1) * DH
                        kv = bank[6][lo:hi, 0:NG * HG * DV].rearrange("p (n j d) -> p n j d", n=NG, j=HG)
                        nc.scalar.mul(KVB[i][lo:hi, :, j, :], kv[:, :, j, :], KS).then_inc(kvb_ready, 1)
                weights(2)
                if has(b, 1):
                    act.wait_ge(cen_ready, b)
                    wait(act, row_out[o], 8 * (b - 1 - o))
                    wait(act, x2t_psum, b - 2)
                    nc.scalar.activation(X2N[o][:].rearrange("p c (h d) -> p (c h) d", h=NH),
                                         TOT[o][:, :, 0:DH], ACT.Square).then_inc(sq_ready, 1)
                if has(b, 3):
                    act.wait_ge(x2t_psum, b - 2)
                    wait(act, score_psum, b - 3)
                    nc.scalar.copy(X2T[:].rearrange("p k s -> p (k s)"), bank[7][:]).then_inc(x2t_ready, 1)
                weights(3)
                if has(b, 2):
                    act.wait_ge(late_steps, 2 * NC * (b - 1))
                    power(rs3[:], lnv3[:], mv3[:, :, 1], 0, var3_log, b - 1, rstd3)
                if has(b, 1):
                    act.wait_ge(z_ready, b)
                    power(zp[:], lnz[:], z2[:], 1, z_log, b, zpow_ready)
                if has(b, 0):
                    high(b + B, wst[i][:], IN1 + 8 * (b - i) + 16, wst_in[i])
            mixing(act, step)

            act.wait_ge(r_diff, 1)
            nc.scalar.activation(ex[:], first[:], ACT.Exp).then_inc(r_exp, 1)

            def expert(j, x):
                i, o = x % 2, 1 - x % 2
                up, ahead, down = stages(j)
                if up:
                    act.wait_ge(up_ready, 2 * j + 1)
                    wait(act, hd_ready, j - 1)
                    nc.scalar.activation(SG[i][:], bank[2 * i][:], ACT.Silu).then_inc(sg_ready, 1)
                if down:
                    act.wait_ge(ht_psum, j)
                    wait(act, y_psum, j - 2)
                    nc.scalar.copy(HTH[o][:].rearrange("p k s -> p (k s)"), bank[5][:]).then_inc(hth_ready, 1)
                if ahead:
                    act.wait_ge(xt_psum, j + 2)
                    wait(act, up_ready, 2 * j)
                    nc.scalar.copy(XH[o][:].rearrange("p k s -> p (k s)"), bank[4][:, 0:E]).then_inc(xh_ready, 1)
                if up:
                    e = act.value_load(etab[0:1, bass.ds(j, 1)], min_val=0, max_val=NE - 1)
                    wait(act, y_psum, j - 1)
                    nc.scalar.copy(W3H[i][:], w3[:, bass.ds(e, 1)].rearrange("p a k d -> p (a k d)")
                                   ).then_inc(w3h_ready, 1)
                if ahead:
                    weigh(j + 1, (x + 1) % NX)

            def weigh(j, x):
                act.wait_ge(xg_in[x], (16 // NX) * (j - x) + 16)
                wait(act, ys_ready, j - NX + 1)
                e = act.value_load(etab[0:1, bass.ds(j, 1)], min_val=0, max_val=NE - 1)
                nc.scalar.copy(PC[x][:], XG[x][:, bass.ds(e + E, 1)]).then_inc(pc_ready, 1)

            act.wait_ge(tables, 1)
            act.wait_ge(w3_in, 16 * NE)
            act.wait_ge(xt_psum, 1)
            nc.scalar.copy(XH[0][:].rearrange("p k s -> p (k s)"), bank[4][:, 0:E]).then_inc(xh_ready, 1)
            weigh(0, 0)
            expert_tiles(act, expert)

        @block.vector
        def _(dve):
            v = nc.vector
            v.memset(zeros[:], 0.0).then_inc(pair_dve, 1)
            v.memset(eps[:, 0:1], LN_EPS)
            v.memset(eps[:, 1:2], HEAD_EPS).then_inc(eps_set, 1)
            v.memset(zrow[:], 0.0).then_inc(zero_rows, 1)
            dve.wait_ge(consts_in, 16 * N_CONST)
            v.tensor_tensor(gc[:], gk[:], gv[:], ALU.add).then_inc(gc_ready, 1)

            def statistics(counter, b, rows_, st_, mv_):
                for c in range(NC):
                    v.bn_stats(st_[:, c, :], rows_[:, c]).then_inc(counter, 1)
                dve.wait_ge(counter, K1 * b + NC)
                dve.sem_inc(dve_carrier, 1)
                for c in range(NC):
                    v.bn_aggr(mv_[:, c, :], st_[:, c, :]).then_inc(counter, 1)

            def stage1(b, x):
                if has(b, 0):
                    dve.wait_ge(x1_in[x], 4 * (b - x) + 16)
                    statistics(ln1_steps, b, X1[x], st1[x], mv1[x])
                if has(b, 1):
                    a_, y, o = b - 1, (x - 1) % 4, 1 - x % 2
                    dve.wait_ge(ln1_rstd, a_ + 1)
                    wait(dve, qT_psum, a_ - 1)
                    for c in range(NC):
                        ins = v.tensor_scalar(Q1[o][:, c, :], X1[y][:, c, :], mv1[y][:, c, 0:1],
                                              rs1[y][:, c:c + 1], ALU.subtract, ALU.mult)
                    ins.then_inc(q_ready, 1)
            gating(dve, stage1)
            for i in range(2):
                v.memset(QBD[i][:], 0.0)
                ins = v.memset(KVB[i][:], 0.0)
            ins.then_inc(zeroed, 1)
            dve.wait_ge(late_consts, 16 * N_LATE)

            st = Steps(dve, pair_dve, 1)
            dve.wait_ge(pair_in, 32)
            dve.wait_ge(pair_dve, 1)
            st.then(v.tensor_scalar(fm[:], gf[:], fb[:, 0:1], 0.0, ALU.add, ALU.min))
            dve.wait_ge(log_ready, 1)
            st.then(v.tensor_tensor(lsg[:], fm[:], fl[:], ALU.subtract))
            st.then(v.tensor_tensor_scan(cs[:], lsg[:], zeros[:], 0.0, ALU.add, ALU.add))
            st.then(v.scalar_tensor_tensor(g[:], gi[:], ib[:, 0:1], cs[:], ALU.add, ALU.subtract))
            dve.sem_inc(g_there, 1)
            st.then(v.tensor_tensor_scan(M[:], g[:], g[:], -3.0e38, ALU.max, ALU.max))
            st.then(v.tensor_scalar(negM[:], M[:], -1.0, None, ALU.mult))
            v.tensor_tensor(mx[:], cs[:], M[:], ALU.add).then_inc(g_ready, 1)
            three_parts(dve, v, negM, 0, m_parts)
            dve.wait_ge(cols_psum, 1)
            v.tensor_copy(cols[:].rearrange("p a q -> p (a q)"), bank[0][:]).then_inc(cols_ready, 1)
            routing = Steps(dve, r_steps, 0)
            EARLY = NC * (B - 1)

            def te(t):
                return t[:].rearrange("p (t e) -> p t e", e=NE)

            def top2(lo, hi):
                cut = slice(lo, hi)
                io_e = io[:, 0:NE].unsqueeze(1).broadcast_to([P, hi - lo, NE])

                def over_e(t):
                    return t[:, cut].unsqueeze(2).broadcast_to([P, hi - lo, NE])

                def argmax(src, best, onehot):
                    routing.then(v.tensor_reduce(best[:, cut], src, AX.X, ALU.max))
                    routing.then(v.tensor_tensor(te(ta)[:, cut], src, over_e(best), ALU.is_equal))
                    routing.then(v.scalar_tensor_tensor(te(tb)[:, cut], te(ta)[:, cut], float(-NE), io_e,
                                                   ALU.mult, ALU.add))
                    routing.then(v.tensor_reduce(first[:, cut], te(tb)[:, cut], AX.X, ALU.min))
                    routing.then(v.tensor_tensor(te(onehot)[:, cut], te(tb)[:, cut], over_e(first), ALU.is_equal))

                argmax(scores[:, cut], m1, oh1)
                routing.then(v.scalar_tensor_tensor(te(s2)[:, cut], te(oh1)[:, cut], -3.0e38, scores[:, cut],
                                               ALU.mult, ALU.add))
                argmax(te(s2)[:, cut], m2, oh2)

            K3 = 7

            def heads(t):
                return t[:].unsqueeze(2).broadcast_to([P, NC * NH, DH])

            def step(b, i):
                pb, lb, o = b - 1, b - 2, 1 - i
                main, post, late = has(b, 0), has(b, 1), has(b, 2)
                st = Steps(dve, post_steps, K3 * pb)
                tot_ = TOT[o]
                vals = tot_[:, :, 0:DH]

                def combine(n):
                    if main:
                        k = b * 2 * NG + n
                        dve.wait_ge(s_ready, k + 1)
                        dve.wait_ge(d_ready, k + 1)
                        wait(dve, pv_group, k - 1)
                        v.scalar_tensor_tensor(C[n % 2][:], bank[2 + n % 2][:], KS, D[n % 2][:],
                                               ALU.mult, ALU.mult).then_inc(c_ready, 1)

                if isinstance(b, int) and b == B + 1:
                    last_vals = TOT[i][:, :, 0:DH]
                    tail = Steps(dve, tail_steps, 0)
                    dve.wait_ge(sc_ready, B)
                    tail.then(v.tensor_tensor(last_vals, last_vals, heads(sc), ALU.mult))
                    tail.then(v.tensor_tensor(last_vals.rearrange("p (c h) d -> p c h d", c=NC),
                                              last_vals.rearrange("p (c h) d -> p c h d", c=NC),
                                              onwb[:].unsqueeze(1).broadcast_to([P, NC, NH, DH]), ALU.mult))
                    dve.wait_ge(inx[i], 16 * (B // 2))
                    rows_ = X[i][:].rearrange("p c h d -> p (c h) d")
                    v.tensor_tensor(rows_, rows_, last_vals, ALU.add).then_inc(x2_ready, 1)
                combine(0)
                combine(1)
                if post:
                    dve.wait_ge(inter_ready, pb + 1)
                    wait(dve, x2_ready, pb - 1)
                    fac = cols[:, 1, bass.ds(pb * NH, NH)].unsqueeze(2).broadcast_to([P, NH, DV])
                    st.then(v.tensor_tensor(tot_[:, NH:, :], bank[7][:, 0:NH * DV].rearrange("p (h d) -> p h d", h=NH),
                                            fac, ALU.mult))
                    v.tensor_tensor(tot_[:, NH:, :], tot_[:, NH:, :],
                                    bank[5][:, 0:NH * DV].rearrange("p (h d) -> p h d", h=NH),
                                    ALU.add).then_inc(o1_taken, 1)
                if post:
                    dve.wait_ge(o1_taken, pb + 1)
                    dve.wait_ge(o0_taken, pb + 1)
                    sums = tot_[:, :, DH]
                    st.then(v.scalar_tensor_tensor(wabs[:], sums, -1.0, sums, ALU.mult, ALU.max))
                    st.then(v.tensor_tensor(wmax[:].rearrange("p (c h) -> p c h", c=NC),
                                            wabs[:].rearrange("p (c h) -> p c h", c=NC),
                                            cols[:, 2:4, bass.ds(pb * NH, NH)], ALU.max))
                    st.then(v.tensor_scalar(wden[:], wmax[:], NORM_EPS, None, ALU.add))
                    v.reciprocal(rec[:], wden[:])
                    st.then(v.tensor_reduce(mu[:], vals, AX.X, ALU.add))
                    v.scalar_tensor_tensor(vals, heads(mu), -1.0 / DH, vals, ALU.mult, ALU.add
                                           ).then_inc(cen_ready, 1)
                combine(2)
                if late:
                    dve.wait_ge(x2_ready, lb + 1)
                    statistics(late_steps, lb, X[i][:].rearrange("p c h d -> p c (h d)"), st3, mv3)
                if post:
                    dve.wait_ge(sq_ready, pb + 1)
                    st.then(v.tensor_reduce(var[:], X2N[o][:].rearrange("p c (h d) -> p (c h) d", h=NH), AX.X, ALU.add))
                    st.then(v.scalar_tensor_tensor(z[:], var[:], 1.0 / DH, rec[:], ALU.mult, ALU.mult))
                    v.tensor_tensor(z2[:], z[:], rec[:], ALU.mult).then_inc(z_ready, 1)
                combine(3)
                if late:
                    dve.wait_ge(rstd3, lb + 1)
                    wait(dve, row_out[i], 8 * (lb - i))
                    for c in range(NC):
                        ins = v.tensor_scalar(X2N[i][:, c, :], X[i][:, c].rearrange("p h d -> p (h d)"),
                                              mv3[:, c, 0:1], rs3[:, c:c + 1], ALU.subtract, ALU.mult)
                    ins.then_inc(x2n_ready, 1)
                if post:
                    dve.wait_ge(zpow_ready, pb + 1)
                    wait(dve, y_done, pb)
                    v.tensor_tensor(sc[:], rec[:], zp[:], ALU.mult).then_inc(sc_ready, 1)
                    assert st.n == K3, st.n
                if isinstance(b, int) and b == B + 2:
                    dve.wait_ge(score_ready, B - 1)
                    dve.wait_ge(inter_ready, B)
                    top2(0, EARLY)
                if has(b, 3):
                    dve.wait_ge(score_psum, b - 2)
                    v.tensor_copy(scores[:, bass.ds((b - 3) * NC, NC), :],
                                  bank[6][:, NH * DV:NH * DV + NC * NE].rearrange("p (c e) -> p c e", c=NC)
                                  ).then_inc(score_ready, 1)
            mixing(dve, step)

            st = routing

            def over_all(t):
                return t[:].unsqueeze(2).broadcast_to([P, NT, NE])

            def probabilities():
                v.tensor_tensor(first[:], m2[:], m1[:], ALU.subtract).then_inc(r_diff, 1)
                dve.wait_ge(r_exp, 1)
                st.then(v.tensor_scalar(den2[:], ex[:], 1.0, None, ALU.add))
                st.then(v.reciprocal(p1[:], den2[:]))
                st.then(v.tensor_tensor(p2[:], ex[:], p1[:], ALU.mult))
                st.then(v.tensor_tensor(te(ta), te(oh1), over_all(p1), ALU.mult))
                st.then(v.tensor_tensor(te(tb), te(oh2), over_all(p2), ALU.mult))
                v.tensor_tensor(pw[:], ta[:], tb[:], ALU.add).then_inc(probs_ready, 1)

            def tile_experts():
                st.then(v.tensor_tensor(later[:].rearrange("p (t e) -> p t e", e=NE - 1),
                                        io[:, 0:TILES].unsqueeze(2).broadcast_to([P, TILES, NE - 1]),
                                        base[:, 1:NE].unsqueeze(1).broadcast_to([P, TILES, NE - 1]), ALU.is_ge))
                st.then(v.tensor_reduce(count[:], later[:].rearrange("p (t e) -> p t e", e=NE - 1), AX.X, ALU.add))
                st.then(v.tensor_copy(etab[:], count[:]))

            v.memset(zer[:], 0.0)
            dve.wait_ge(score_ready, B)
            for i in range(2):
                dve.wait_ge(x_out[i], 16 * (B // 2))
                dve.wait_ge(row_out[i], 16 * (B // 2))
            top2(EARLY, NT)
            v.tensor_tensor(abf[:], oh1[:], oh2[:], ALU.add).then_inc(r_ones, 1)

            dve.wait_ge(r_counts, 1)
            rank = bank[0][:, 0:SCN]
            tot = bank[0][:, SCN:2 * SCN]
            for e in range(NE):
                ins = v.tensor_tensor_scan(te(cum)[:, :, e], tot.rearrange("p (t e) -> p t e", e=NE)[:, :, e], zer[:],
                                           0.0, ALU.add, ALU.add)
            st.then(ins)
            st.then(v.tensor_scalar(nei[:], te(cum)[:, NT - 1, :], float(P - 1), None, ALU.add))
            st.then(v.tensor_scalar(neb[:], nei[:], 7, None, ALU.arith_shift_right))
            st.then(v.tensor_copy(nef[:], neb[:]))
            st.then(v.memset(base[:, 0:1], 0.0))
            st.then(v.tensor_tensor_scan(base[:, 1:], nef[:], zer[:, 0:NE], 0.0, ALU.add, ALU.add))
            st.then(v.tensor_tensor(slotS[:], cum[:], tot, ALU.subtract))
            st.then(v.tensor_tensor(slotS[:], slotS[:], rank, ALU.add))
            st.then(v.scalar_tensor_tensor(te(slotS), base[:, 0:NE].unsqueeze(1).broadcast_to([P, NT, NE]), float(P),
                                           te(slotS), ALU.mult, ALU.add))
            for k, oh in enumerate((oh1, oh2)):
                st.then(v.tensor_tensor(ta[:], oh[:], slotS[:], ALU.mult))
                st.then(v.tensor_reduce(slot[:].rearrange("p (t k) -> p t k", k=TOPK)[:, :, k], te(ta), AX.X, ALU.add))
            st.then(v.tensor_copy(sloti[:], slot[:]))
            v.tensor_scalar(sj[:], sloti[:], 7, None, ALU.arith_shift_right)
            st.then(v.tensor_scalar(sp_[:], sloti[:], P - 1, None, ALU.bitwise_and))
            v.tensor_copy(jf[:], sj[:])
            st.then(v.tensor_copy(pf[:], sp_[:]))
            def hots(m, i):
                at = bass.ds(m * NI, NI)
                wait(dve, inverted, m - 3)
                v.tensor_tensor(OHP[i][:].rearrange("p (n q) -> p n q", n=NI),
                                io[:, 0:P].unsqueeze(1).broadcast_to([P, NI, P]),
                                pf[:, at].unsqueeze(2).broadcast_to([P, NI, P]), ALU.is_equal)
                v.tensor_tensor(OHJ[i][:].rearrange("p (n j) -> p n j", n=NI),
                                io[:, 0:TILES].unsqueeze(1).broadcast_to([P, NI, TILES]),
                                jf[:, at].unsqueeze(2).broadcast_to([P, NI, TILES]),
                                ALU.is_equal).then_inc(hots_made, 1)
                if isinstance(m, int) and m == TOPK * NT // NI - 4:
                    probabilities()
            inversion(dve, hots)
            tile_experts()
            dve.wait_ge(inverted, TOPK * NT // NI)
            st.then(v.tensor_scalar(fil[:], bank[1][:, TILES:2 * TILES], 0.0, io[:, P:P + 1], ALU.is_equal, ALU.mult))
            st.then(v.scalar_tensor_tensor(count[:], bank[1][:, TILES:2 * TILES], float(P), fil[:], ALU.mult, ALU.add))
            st.then(v.tensor_tensor(count[:], count[:], bank[1][:, 0:TILES], ALU.add))
            v.tensor_scalar(index[:], count[:], float(-P), None, ALU.add).then_inc(tables, 1)

            def low(j, i):
                dve.wait_ge(xh_ready, j + 1)
                wait(dve, up_ready, 2 * (j - 1))
                v.tensor_tensor(XL[i][:].rearrange("p k s -> p (k s)"), bank[4][:, 0:E],
                                XH[i][:].bitcast(F32).rearrange("p k s -> p (k s)"),
                                ALU.subtract).then_inc(xl_ready, 1)

            def expert(j, x):
                i, o = x % 2, 1 - x % 2
                up, ahead, down = stages(j)
                if down:
                    dve.wait_ge(hth_ready, j)
                    wait(dve, y_psum, j - 2)
                    v.tensor_tensor(HTL[o][:].rearrange("p k s -> p (k s)"), bank[5][:],
                                    HTH[o][:].bitcast(F32).rearrange("p k s -> p (k s)"),
                                    ALU.subtract).then_inc(htl_ready, 1)
                if up:
                    dve.wait_ge(sg_ready, j + 1)
                    dve.wait_ge(up_ready, 2 * (j + 1))
                    wait(dve, ht_psum, j - 1)
                    v.tensor_tensor(HD[i][:], SG[i][:], bank[2 * i + 1][:], ALU.mult).then_inc(hd_ready, 1)
                if ahead:
                    low(j + 1, 1 - i)
                if down:
                    dve.wait_ge(y_psum, j)
                    dve.wait_ge(pc_ready, j)
                    wait(dve, y_added, 16 * (j - 2))
                    v.tensor_scalar(YS[o][:], bank[6][:, 0:E], PC[(x - 1) % NX][:, 0:1], None, ALU.mult).then_inc(ys_ready, 1)
                if up:
                    e = dve.value_load(etab[0:1, bass.ds(j, 1)], min_val=0, max_val=NE - 1)
                    dve.wait_ge(w3h_ready, j + 1)
                    wait(dve, y_psum, j - 1)
                    v.tensor_tensor(W3L[i][:], w3[:, bass.ds(e, 1)].rearrange("p a k d -> p (a k d)"),
                                    W3H[i][:].bitcast(F32), ALU.subtract).then_inc(w3l_ready, 1)
            low(0, 0)
            dve.wait_ge(w3_in, 16 * NE)
            dve.wait_ge(tables, 1)
            expert_tiles(dve, expert)

        @block.gpsimd
        def _(pool):
            q = nc.gpsimd

            def low(piece, src, count, steps=1):
                pool.wait_ge(w_hi, count)
                at = bass.ds(piece * HID, HID)
                q.tensor_tensor(w12l[:].rearrange("p e k h -> p (e k h)")[:, at], src,
                                w12h[:].bitcast(F32).rearrange("p e k h -> p (e k h)")[:, at],
                                ALU.subtract).then_inc(w_lo, steps)

            def load_w(piece, i, count):
                wait(pool, w_lo, count)
                pool.sem_inc(pool_carrier, 1)
                q.dma_start(wst[i][:], w12T[:, bass.ds(piece * HID, HID)]).then_inc(wst_in[i], 16)

            def stage1(b, x):
                if x % 2:
                    if has(b, 0):
                        load_w(b, x // 2, max(b - 1, 1) if isinstance(b, int) else b - 1)
                    if has(b, 2):
                        low(b - 2, wst[(x - 2) % 4 // 2][:], W0 + b - 1, steps=2)
            for n, piece in enumerate(PIECES0):
                load_w(piece, n, 0)
            for n, piece in enumerate(PIECES0):
                low(piece, wst[n][:], n + 1)
            gating(pool, stage1)
            for n in range(EARLY2):
                low(PIECES2[n], BUF2[n], W1 + n + 1)

            pool.wait_ge(g_there, 1)
            pool.sem_inc(g_rest, 1)
            for k in range(PARTS - 1):
                pool.wait_ge(g_parts, k + 1)
                src = g[:] if k == 0 else rest[:, 1, k - 1, :]
                q.tensor_tensor(rest[:, 1, k, :], src, parts[:, 1, k, :], ALU.subtract).then_inc(g_rest, 1)
            for n in range(EARLY2, len(PIECES2)):
                low(PIECES2[n], BUF2[n], W1 + n + 1)
            pool.wait_ge(cols_ready, 1)

            def step(b, i):
                pb, o = b - 2, 1 - i
                if has(b, 0):
                    pool.wait_ge(inv3[i], loaded(b, i, LOADSV))
                    wait(pool, inter_ready, b - 1)
                    q.tensor_tensor(VW[i][:], AUG[i][:, 0],
                                    cols[:, 0, bass.ds(b * NH, NH)].unsqueeze(2).broadcast_to([P, NH, DV]),
                                    ALU.mult).then_inc(vw_ready, 1)
                if has(b, 2) and not (isinstance(b, int) and b == B + 1):
                    parts_ = [TOT[i][:, c * NH:(c + 1) * NH, 0:DH] for c in range(NC)]
                    pool.wait_ge(sc_ready, pb + 1)
                    for c in range(NC):
                        ins = q.tensor_tensor(parts_[c], parts_[c], sc[:, c * NH:(c + 1) * NH].unsqueeze(2)
                                              .broadcast_to([P, NH, DH]), ALU.mult).then_inc(mix_steps, 1)
                    for c in range(NC):
                        pool.wait_ge(mix_steps, 2 * NC * pb + c + 1)
                        if c == NC - 1:
                            pool.sem_inc(y_done, 1)
                        q.tensor_tensor(parts_[c], parts_[c], onwb[:], ALU.mult).then_inc(mix_steps, 1)
                    pool.wait_ge(inx[i], 8 * (pb - i) + 16)
                    for c in range(NC):
                        pool.wait_ge(mix_steps, 2 * NC * pb + NC + c + 1)
                        ins = q.tensor_tensor(X[i][:, c], X[i][:, c], parts_[c], ALU.add)
                    ins.then_inc(x2_ready, 1)
                if has(b, 0):
                    load_w(b + B, i, W2 - 1 + b)
                if has(b, 1):
                    low(b - 1 + B, wst[o][:], W2 + b)
            mixing(pool, step)

            def number(m, i):
                pool.wait_ge(hots_made, m + 1)
                wait(pool, inverted, m - 3)
                q.tensor_tensor(OHN[i][:].rearrange("p (n a j) -> p n a j", n=NI, a=2),
                                OHJ[i][:].rearrange("p (n j) -> p n j", n=NI).unsqueeze(2)
                                .broadcast_to([P, NI, 2, TILES]),
                                numbers[:, bass.ds(m * (2 * NI), 2 * NI)].rearrange("p (n a) -> p n a", a=2)
                                .unsqueeze(3).broadcast_to([P, NI, 2, TILES]), ALU.mult).then_inc(hots_ready, 1)
            inversion(pool, number)

            def gather(j, x):
                wait(pool, xt_psum, j - NX + 1)
                wait(pool, pc_ready, j - NX + 1)
                pool.sem_inc(pool_carrier, 1)
                q.tensor_copy(IXG[x][:], index[:, bass.ds(j, 1)]).then_inc(ixg_ready, 1)
                pool.wait_ge(ixg_ready, j + 1)
                pool.sem_inc(pool_carrier, 1)
                q.indirect_dma_start(out=XG[x][:], out_offset=None, in_=table,
                                     in_offset=bass.IndirectOffsetOnAxis(ap=IXG[x][:, 0:1], axis=0)
                                     ).then_inc(xg_in[x], 16)

            def add(j, i):
                wait(pool, y_added, 16 * j)
                pool.sem_inc(pool_carrier, 1)
                q.tensor_copy(IXS[i][:], index[:, bass.ds(j, 1)]).then_inc(ixs_ready, 1)
                pool.wait_ge(ixs_ready, j + 1)
                pool.wait_ge(ys_ready, j + 1)
                pool.sem_inc(pool_carrier, 1)
                q.indirect_dma_start(out=out, out_offset=bass.IndirectOffsetOnAxis(ap=IXS[i][:, 0:1], axis=0),
                                     in_=YS[i][:], in_offset=None, compute_op=ALU.add).then_inc(y_added, 16)

            def expert(j, x):
                if not isinstance(j, int) or j + NX - 1 < TILES:
                    gather(j + NX - 1, (x - 1) % NX)
                if stages(j)[2]:
                    add(j - 1, 1 - x % 2)

            pool.wait_ge(tables, 1)
            pool.wait_ge(probs_out, 16)
            for i in range(2):
                pool.wait_ge(x_out[i], 16 * (B // 2))
                pool.wait_ge(row_out[i], 16 * (B // 2))
            pool.wait_ge(zero_out, 32)
            for x in range(NX - 1):
                gather(x, x)
            expert_tiles(pool, expert)
            pool.wait_ge(y_added, 16 * TILES)

        @block.tensor
        def _(pe):
            mm = nc.tensor.matmul
            pe.wait_ge(consts_in, 16 * N_CONST)
            pe.wait_ge(gc_ready, 1)

            def turn(b, i):
                pe.wait_ge(q_ready, b + 1)
                wait(pe, qT_ready, b - 1)
                for k in range(NK):
                    for c in range(NC):
                        ins = nc.tensor.transpose(bank[i][:, k * S + c * P:k * S + (c + 1) * P],
                                                  Q1[i][:, c, k * P:(k + 1) * P], id_f[:])
                ins.then_inc(qT_psum, 1)

            def gates(b, x):
                pe.wait_ge(qT_ready, b + 1)
                pe.wait_ge(ct1_in[x], 4 * (b - x) + 16)
                wait(pe, gates_ready, b - 1)
                i = x % 2
                o = bank[2 + i][0:2 * NH, 0:S]
                for k in range(NK):
                    mm(o, gq[:, k, :], QT1[i][:, k, :], start=(k == 0), stop=False)
                for k in range(NK):
                    ins = mm(o, gc[:, k, :], CT1[x][:, k, :], start=False, stop=(k == NK - 1))
                ins.then_inc(gates_psum, 1)

            def stage1(b, x):
                if has(b, 1):
                    turn(b - 1, 1 - x % 2)
                if has(b, 2):
                    gates(b - 2, (x - 2) % 4)
            gating(pe, stage1)

            pe.wait_ge(dcol_ready, 1)
            for k in range(4):
                ins = nc.tensor.transpose(bank[0][:, k * P:(k + 1) * P], dcol[:, k, :], id_f[:])
            ins.then_inc(cols_psum, 1)
            pe.wait_ge(cols_ready, 1)
            pe.wait_ge(w_lo, W2 - len(wst))
            pe.wait_ge(late_consts, 16 * N_LATE)

            def step(b, i):
                main, last, late, o = has(b, 0), has(b, 1), has(b, 3), 1 - i

                def exponents(n):
                    c, hg = n // NG, n % NG
                    k = b * 2 * NG + n
                    wait(pe, d_ready, k - 1)
                    mm(bank[n % 2][:], LG[i][:, c * P:(c + 1) * P],
                       RM[i][:, hg * HG:(hg + 1) * HG, c * P:(c + 1) * P], start=True, stop=False)
                    mm(bank[n % 2][:], id_b[:], mask4[:], start=False, stop=True).then_inc(e_ready, 1)
                    wait(pe, c_ready, k - 1)
                    mm(bank[2 + n % 2][:], KT[i][:, hg, c * P:(c + 1) * P],
                       QBD[i][:, hg, :, c * P:(c + 1) * P], start=True, stop=True).then_inc(s_ready, 1)

                def values(vb, vi, n):
                    c, hg = n // NG, n % NG
                    pe.wait_ge(c_ready, vb * 2 * NG + n + 1)
                    if n == 0:
                        pe.wait_ge(inv3[vi], loaded(vb, vi, LOADSV))
                        wait(pe, o0_taken, vb)
                    if n == NG:
                        wait(pe, o1_taken, vb)
                    for j in range(HG):
                        h = hg * HG + j
                        ins = mm(bank[4 + c][:, h * DV:(h + 1) * DV], C[n % 2][:, j * P:(j + 1) * P],
                                 AUG[vi][:, c, h, :], start=True, stop=True)
                    ins.then_inc(pv_group, 1)

                if main:
                    pe.wait_ge(in3[i], loaded(b, i, LOADS3))
                    exponents(0)
                if last:
                    values(b - 1, o, 2)
                if main:
                    exponents(1)
                if last:
                    values(b - 1, o, 3)
                    wait(pe, o1_taken, b - 1)
                    wait(pe, x2t_ready, b - 3)
                    for n in range(NG):
                        ins = mm(bank[7][:, n * HG * DV:(n + 1) * HG * DV], QTB[o][:, n, :],
                                 KVB[o][:, n].rearrange("p j d -> p (j d)"), start=True, stop=True)
                    ins.then_inc(inter_ready, 1)
                if main:
                    pe.wait_ge(vw_ready, b + 1)
                    wait(pe, score_ready, b - 3)
                    wait(pe, kvb_ready, HG * b)
                    for n in range(NG):
                        ins = mm(bank[6][:, n * HG * DV:(n + 1) * HG * DV], KN[i][:, n * P:(n + 1) * P],
                                 VW[i][:, n * HG:(n + 1) * HG, :], start=True, stop=True)
                    ins.then_inc(kv_psum, 1)
                    exponents(2)
                    values(b, i, 0)
                if late:
                    pe.wait_ge(x2n_ready, b - 2)
                    pe.wait_ge(o1_taken, min(b, B) if isinstance(b, int) else b)
                    for n in range(NC * NK):
                        ins = nc.tensor.transpose(bank[7][:, n * P:(n + 1) * P],
                                                  X2N[o][:, n // NK, n % NK * P:(n % NK + 1) * P], id_f[:])
                    ins.then_inc(x2t_psum, 1)
                if main:
                    exponents(3)
                    values(b, i, 1)
                if late:
                    pe.wait_ge(x2t_ready, b - 2)
                    wait(pe, score_ready, b - 3)
                    pe.wait_ge(kvb_ready, min(HG * (b + 1), HG * B) if isinstance(b, int) else HG * (b + 1))
                    for c in range(NC):
                        at = NH * DV + c * NE
                        for k in range(NK):
                            ins = mm(bank[6][:, at:at + NE], X2T[:, c * NK + k, :], gate_w[:, k, :],
                                     start=(k == 0), stop=(k == NK - 1))
                    ins.then_inc(score_psum, 1)
            mixing(pe, step)

            pe.wait_ge(r_ones, 1)
            mm(bank[0][:, 0:SCN], tri[:, 0, :], abf[:], start=True, stop=True)
            mm(bank[0][:, SCN:2 * SCN], tri[:, 1, :], abf[:], start=True, stop=True).then_inc(r_counts, 1)

            def invert(m, i):
                first, end = isinstance(m, int) and m == 0, isinstance(m, int) and m == TOPK * NT // NI - 1
                pe.wait_ge(hots_ready, m + 1)
                for k in range(NI):
                    ins = mm(bank[1][:, 0:2 * TILES], OHP[i][:, k * P:(k + 1) * P],
                             OHN[i][:, k * 2 * TILES:(k + 1) * 2 * TILES], start=first and k == 0, stop=end and k == NI - 1)
                ins.then_inc(inverted, 1)
            inversion(pe, invert)

            def rows(j, x):
                pe.wait_ge(xg_in[x], (16 // NX) * (j - x) + 16)
                wait(pe, xl_ready, j)
                for k in range(NK):
                    ins = nc.tensor.transpose(bank[4][:, k * P:(k + 1) * P], XG[x][:, k * P:(k + 1) * P], id_f[:])
                ins.then_inc(xt_psum, 1)

            def expert(j, x):
                i, o = x % 2, 1 - x % 2
                up, ahead, down = stages(j)

                def half_up(half):
                    acc = bank[2 * i + half][:]
                    for k in range(NK):
                        wh = w12h[:, bass.ds(e, 1), k, half * HID:(half + 1) * HID].rearrange("p a h -> p (a h)")
                        wl = w12l[:, bass.ds(e, 1), k, half * HID:(half + 1) * HID].rearrange("p a h -> p (a h)")
                        mm(acc, XH[i][:, k, :], wl, start=(k == 0), stop=False)
                        mm(acc, XL[i][:, k, :], wh, start=False, stop=False)
                        ins = mm(acc, XH[i][:, k, :], wh, start=False, stop=(k == NK - 1))
                    ins.then_inc(up_ready, 1)

                if up:
                    e = pe.value_load(etab[0:1, bass.ds(j, 1)], min_val=0, max_val=NE - 1)
                    pe.wait_ge(xl_ready, j + 1)
                    wait(pe, hd_ready, j - 1)
                    half_up(0)
                if down:
                    pe.wait_ge(hd_ready, j)
                    wait(pe, htl_ready, j - 1)
                    for k in range(KH):
                        ins = nc.tensor.transpose(bank[5][:, k * P:(k + 1) * P], HD[o][:, k * P:(k + 1) * P], id_f[:])
                    ins.then_inc(ht_psum, 1)
                if up:
                    half_up(1)
                if ahead:
                    rows(j + 1, (x + 1) % NX)
                if down:
                    acc = bank[6][:, 0:E]
                    pe.wait_ge(hth_ready, j)
                    pe.wait_ge(w3l_ready, j)
                    wait(pe, ys_ready, j - 1)
                    for k in range(KH):
                        mm(acc, HTH[o][:, k, :], W3L[o][:, k * E:(k + 1) * E], start=(k == 0), stop=False)
                        mm(acc, HTH[o][:, k, :], W3H[o][:, k * E:(k + 1) * E], start=False, stop=False)
                    pe.wait_ge(htl_ready, j)
                    for k in range(KH):
                        ins = mm(acc, HTL[o][:, k, :], W3H[o][:, k * E:(k + 1) * E], start=False, stop=(k == KH - 1))
                    ins.then_inc(y_psum, 1)

            pe.wait_ge(tables, 1)
            rows(0, 0)
            expert_tiles(pe, expert)


_OUT = (ROWS, E)


def kernel(x, ctx_1024, L0_xattn_igate_kernel, L0_xattn_igate_bias, L0_xattn_fgate_kernel,
           L0_xattn_fgate_bias, L0_xattn_outnorm_weight, L0_ffn_w12, L0_ffn_w3, L0_ffn_gate_w):
    import ml_dtypes
    import concourse.bacc as bacc
    from concourse.bass_utils import run_bass_kernel_spmd as run

    bf = ml_dtypes.bfloat16
    a = {k: np.asarray(v) for k, v in dict(
        x=x, ctx=ctx_1024, ik=L0_xattn_igate_kernel, ib=L0_xattn_igate_bias, fk=L0_xattn_fgate_kernel,
        fb=L0_xattn_fgate_bias, onw=L0_xattn_outnorm_weight, w12=L0_ffn_w12, w3=L0_ffn_w3,
        gate=L0_ffn_gate_w).items()}
    ctx2 = a["ctx"].reshape(N, E)
    gk = np.concatenate([a["ik"], a["fk"]], axis=1).reshape(3, NK, P, 2 * NH).transpose(0, 2, 1, 3).reshape(3, P, -1)
    p, q = np.arange(P)[:, None], np.arange(P)[None, :]
    marks = np.ones((PARTS * (NH + 1), NH * S), np.float32)
    marks[PARTS:] = np.tile(np.repeat(np.eye(NH), S, axis=1), (PARTS, 1))
    ins = {
        "x": a["x"].reshape(N, E),
        "ctx": ctx2,
        "ctxv": np.concatenate([ctx2.reshape(N, NH, DH), np.ones((N, NH, 1), np.float32)], axis=2).reshape(N, NH * DV),
        "ctxT": ctx2.T,
        "gkq": gk[0], "gkk": gk[1], "gkv": gk[2],
        "ibias": np.tile(a["ib"], B)[:, None],
        "fbias": np.tile(a["fb"], B)[:, None],
        "onw": np.broadcast_to(a["onw"].reshape(1, E), (P, E)),
        "w12T": a["w12"].transpose(2, 0, 1).reshape(NK, P, NE, 2 * HID).transpose(1, 2, 0, 3).reshape(P, -1),
        "w3T": a["w3"].transpose(2, 0, 1).reshape(KH, P, NE, E).transpose(1, 2, 0, 3).reshape(P, -1),
        "gateT": a["gate"].T.reshape(NK, P, NE).transpose(1, 0, 2).reshape(P, -1),
        "ident": np.eye(P, dtype=np.float32),
        "identb": np.eye(P).astype(bf),
        "maskT": np.tile(np.where(p > q, MASKED, 0.0), (1, HG)).astype(bf),
        "trib": np.concatenate([p < q, np.ones((P, P))], axis=1).astype(bf),
        "marks": marks.astype(bf),
        "iota": np.concatenate([np.broadcast_to(q, (P, P)), N + P + p], axis=1).astype(np.float32),
        "nums": np.stack(np.broadcast_arrays(p, 1 + np.repeat(np.arange(NT), TOPK)[None, :]),
                         axis=2).reshape(P, -1).astype(np.float32),
    }
    nc = bacc.Bacc("TRN2", target_bir_lowering=False, num_devices=1)
    arrays, args = {}, []
    for name, v in ins.items():
        arrays["in_" + name] = np.ascontiguousarray(v)
        args.append(nc.dram_tensor("in_" + name, v.shape, mybir.dt.from_np(v.dtype), kind="ExternalInput").ap())
    args.append(nc.dram_tensor("out_rows", _OUT, F32, kind="ExternalOutput").ap())
    build(nc, *args)
    r = run(nc, [arrays], core_ids=[0])
    return r.results[0]["out_rows"][0:N].reshape(B, S, E)
```
